# Optimizing a Trainium2 kernel written in Bass

```python
import numpy as np
import jax
import jax.numpy as jnp

def _softmax(x, axis=-1):
    return jax.nn.softmax(x, axis=axis)

def _gelu(x):
    return jax.nn.gelu(x, approximate=True)

def _silu(x):
    return jax.nn.silu(x)

def _sigmoid(x):
    return jax.nn.sigmoid(x)

def _layernorm(x, axis=-1, eps=1e-05):
    m = jnp.mean(x, axis=axis, keepdims=True)
    v = jnp.var(x, axis=axis, keepdims=True)
    return (x - m) / jnp.sqrt(v + eps)

def _scatter_add(tgt, idx, src, axis=0):
    return tgt.at[idx].add(src)

def _segment_sum(src, seg, n):
    return jax.ops.segment_sum(src, seg, n)
kernel_name = 'mk_seq_preln_d1_jaxref_r8_98e748'

def setup_inputs(seed: int=0):
    np.random.seed(seed)
    _w = jnp.asarray

    def _L0_attn_setup():
        import jax, jax.numpy as jnp
        import numpy as np
        FEATS = 128
        HEAD = 16
        HEAD_DIM = FEATS // HEAD
        EPS = 1e-12

        def _l2norm(t):
            n = jnp.sqrt(jnp.sum(t * t, axis=-1, keepdims=True))
            return t / jnp.maximum(n, EPS)
        key = jax.random.key(seed)
        ks = jax.random.split(key, 10)
        s = 0.02
        inp = {'x': jax.random.normal(ks[0], (4, 256, FEATS), dtype=jnp.float32), 'Wq': jax.random.normal(ks[1], (FEATS, FEATS), dtype=jnp.float32) * s, 'bq': jnp.zeros((FEATS,), dtype=jnp.float32), 'Wk': jax.random.normal(ks[2], (FEATS, FEATS), dtype=jnp.float32) * s, 'bk': jnp.zeros((FEATS,), dtype=jnp.float32), 'Wv': jax.random.normal(ks[3], (FEATS, FEATS), dtype=jnp.float32) * s, 'bv': jnp.zeros((FEATS,), dtype=jnp.float32), 'Wo': jax.random.normal(ks[4], (FEATS, FEATS), dtype=jnp.float32) * s, 'bo': jnp.zeros((FEATS,), dtype=jnp.float32), 'm': jnp.full((HEAD,), 0.5, dtype=jnp.float32)}
        return inp
    _L0_attn_in = _L0_attn_setup()

    def _L0_ffn_setup():
        import jax, jax.numpy as jnp
        import numpy as np
        B, S, H, E, K = (4, 256, 128, 8, 2)
        F = 4 * H
        key = jax.random.key(seed)
        ks = jax.random.split(key, 6)
        s_h = 1.0 / np.sqrt(H)
        s_f = 1.0 / np.sqrt(F)
        return {'x': jax.random.normal(ks[0], (B, S, H), dtype=jnp.float32), 'Wg': jax.random.uniform(ks[1], (E, H), minval=-s_h, maxval=s_h, dtype=jnp.float32), 'w1': jax.random.uniform(ks[2], (E, H, F), minval=-s_h, maxval=s_h, dtype=jnp.float32), 'b1': jax.random.uniform(ks[3], (E, F), minval=-s_h, maxval=s_h, dtype=jnp.float32), 'w2': jax.random.uniform(ks[4], (E, F, H), minval=-s_f, maxval=s_f, dtype=jnp.float32), 'b2': jax.random.uniform(ks[5], (E, H), minval=-s_f, maxval=s_f, dtype=jnp.float32)}
    _L0_ffn_in = _L0_ffn_setup()
    _d = {'L0_attn_x': _L0_attn_in['x'], 'L0_attn_Wq': _L0_attn_in['Wq'], 'L0_attn_bq': _L0_attn_in['bq'], 'L0_attn_Wk': _L0_attn_in['Wk'], 'L0_attn_bk': _L0_attn_in['bk'], 'L0_attn_Wv': _L0_attn_in['Wv'], 'L0_attn_bv': _L0_attn_in['bv'], 'L0_attn_Wo': _L0_attn_in['Wo'], 'L0_attn_bo': _L0_attn_in['bo'], 'L0_attn_m': _L0_attn_in['m'], 'L0_ffn_Wg': _L0_ffn_in['Wg'], 'L0_ffn_w1': _L0_ffn_in['w1'], 'L0_ffn_b1': _L0_ffn_in['b1'], 'L0_ffn_w2': _L0_ffn_in['w2'], 'L0_ffn_b2': _L0_ffn_in['b2']}
    _x0 = _d['L0_attn_x']
    _d['L0_attn_x'] = jax.random.normal(jax.random.fold_in(jax.random.key(seed), 1), (16, 256, 128), dtype=_x0.dtype)
    del _x0
    return _d

def reference(L0_attn_x, L0_attn_Wq, L0_attn_bq, L0_attn_Wk, L0_attn_bk, L0_attn_Wv, L0_attn_bv, L0_attn_Wo, L0_attn_bo, L0_attn_m, L0_ffn_Wg, L0_ffn_w1, L0_ffn_b1, L0_ffn_w2, L0_ffn_b2):

    def _L0_attn_ref(x, Wq, bq, Wk, bk, Wv, bv, Wo, bo, m):
        import jax, jax.numpy as jnp
        import numpy as np
        FEATS = 128
        HEAD = 16
        HEAD_DIM = FEATS // HEAD
        EPS = 1e-12

        def _l2norm(t):
            n = jnp.sqrt(jnp.sum(t * t, axis=-1, keepdims=True))
            return t / jnp.maximum(n, EPS)
        b, n, f = x.shape

        def proj(W, bias):
            y = x @ W + bias
            return y.reshape(b, n, HEAD, HEAD_DIM).transpose(0, 2, 1, 3)
        q = _l2norm(proj(Wq, bq))
        k = _l2norm(proj(Wk, bk))
        v = proj(Wv, bv)
        sim = jnp.einsum('bhid,bhjd->bhij', q, k)
        sigma_m = jax.nn.sigmoid(m).reshape(1, HEAD, 1, 1)
        scaling = jnp.asarray(n, dtype=x.dtype) ** sigma_m
        attn = sim / scaling
        out = jnp.einsum('bhij,bhjd->bhid', attn, v)
        out = out.transpose(0, 2, 1, 3).reshape(b, n, f)
        return out @ Wo + bo

    def _L0_ffn_ref(x, Wg, w1, b1, w2, b2):
        import jax, jax.numpy as jnp
        import numpy as np
        B, S, H, E, K = (4, 256, 128, 8, 2)
        F = 4 * H
        logits = jnp.einsum('bsh,eh->bse', jax.lax.stop_gradient(x), Wg)
        probs = jax.nn.softmax(logits, axis=-1)
        topk_w, topk_idx = jax.lax.top_k(probs, K)
        h = jnp.einsum('bsh,ehf->bsef', x, w1) + b1
        h = jax.nn.gelu(h, approximate=False)
        eo = jnp.einsum('bsef,efh->bseh', h, w2) + b2
        sel = jnp.take_along_axis(eo, topk_idx[..., None], axis=2)
        out = jnp.sum(topk_w[..., None] * sel, axis=2)
        return out
    x = L0_attn_x
    x = x + _L0_attn_ref(_layernorm(x, axis=-1), L0_attn_Wq, L0_attn_bq, L0_attn_Wk, L0_attn_bk, L0_attn_Wv, L0_attn_bv, L0_attn_Wo, L0_attn_bo, L0_attn_m)
    x = x + _L0_ffn_ref(_layernorm(x, axis=-1), L0_ffn_Wg, L0_ffn_w1, L0_ffn_b1, L0_ffn_w2, L0_ffn_b2)
    return x

_drawn_inputs = setup_inputs


def setup_inputs(seed=0):
    import zlib

    import numpy as np

    out = dict(_drawn_inputs(seed))
    spreads = {'L0_attn_bq': (0.0, 0.597),
     'L0_attn_bk': (0.0, 0.298),
     'L0_attn_bv': (0.0, 0.297),
     'L0_attn_bo': (0.0, 0.1),
     'L0_attn_m': (0.5, 0.6)}
    factors = {'L0_attn_Wk': 3.393, 'L0_attn_Wv': 3.557, 'L0_ffn_b1': 8.0, 'L0_ffn_b2': 6.768}
    for name, (base, spread) in spreads.items():
        noise = np.random.default_rng([zlib.crc32(name.encode()), seed]).standard_normal(out[name].shape)
        drawn = base * np.exp(spread * noise) if base else spread * noise
        out[name] = jnp.asarray(drawn.astype(out[name].dtype))
    for name, factor in factors.items():
        out[name] = (out[name] * factor).astype(out[name].dtype)
    return out
```

```python
from contextlib import ExitStack

import numpy as np
import concourse.bass as bass
from concourse import mybir

P = 128
F32 = mybir.dt.float32
BF16 = mybir.dt.bfloat16
I32 = mybir.dt.int32
ALU = mybir.AluOpType
ACT = mybir.ActivationFunctionType
AX = mybir.AxisListType.X
LN_EPS = 1e-5
L2_EPS = 1e-12


def moe_block(nc, x, Wq, bq, Wk, bk, Wv, bv, Wo, bo, m, Wg, w1, b1, w2, b2, out, xs, ys):
    NB, S, D = x.shape
    HEADS = m.shape[0]
    HD = D // HEADS
    E, _, F = w1.shape
    FC = F // P
    K = 2
    T = NB * S
    NT = T // P
    G = 4
    NG = NT // G
    BG = G * P // S
    TB = S // P
    REGION = T + P
    ROW = D + 1
    NS = K * NT + E
    U = 8
    SENT_OUT = K * T
    assert D == P and NS % U == 0 and NG % 2 == 0 and NG >= 4 and E == NG

    x_v = x.rearrange("b (u p) f -> p (b u) f", p=P)
    out_v = out.rearrange("b (u p) f -> p (b u) f", p=P)
    ys_v = ys.rearrange("(k t p) f -> p k t f", k=K, p=P)

    with ExitStack() as ctx:
        def sb(name, shape, dt=F32):
            return ctx.enter_context(nc.sbuf_tensor(name, shape, dt))

        def pb(name, shape, dt=F32):
            return ctx.enter_context(nc.psum_tensor(name, shape, dt))

        def sem(name):
            return ctx.enter_context(nc.semaphore(name))

        xin = sb("xin", [P, NT, D])
        x2 = sb("x2", [P, NT, D])
        w1s = sb("w1s", [P, E, F])
        w2s = sb("w2s", [P, E, FC, D])
        b2bc = sb("b2bc", [P, E, D])
        bobc = sb("bobc", [P, D])
        wqk = sb("wqk", [P, 2 * D])
        wv = sb("wv", [P, D])
        wo = sb("wo", [P, D])
        wgrow = sb("wgrow", [E, D])
        wgT = sb("wgT", [P, E])
        brow = sb("brow", [1, 3 * D])
        b1row = sb("b1row", [1, E, F])
        mcol = sb("mcol", [P, 1])
        ident = sb("ident", [P, P])
        headmask = sb("headmask", [P, P])
        negmean = sb("negmean", [P, P])
        onerow = sb("onerow", [1, P])
        tri = sb("tri", [P, P], BF16)
        ones = sb("ones", [P, P], BF16)
        eps = sb("eps", [P, 1])
        rev = sb("rev", [P, G, E])
        revi = sb("revi", [P, G, E], I32)
        regbase = sb("regbase", [P, G, E])
        regbasei = sb("regbasei", [P, G, E], I32)
        dest = sb("dest", [P, NT, K], I32)
        sidx = sb("sidx", [1, NS])
        sidxi = sb("sidxi", [1, NS], I32)
        padrow = sb("padrow", [P, ROW])
        stats = sb("stats", [P, G, 6])
        sv = sb("sv", [P, G, 2])
        md = sb("md", [P, G])
        var = sb("var", [P, G])
        std = sb("std", [P, G])
        rstd = sb("rstd", [P, G])
        mms = sb("mms", [P, G])
        xn = sb("xn", [P, 2, G, D])
        xnT = sb("xnT", [P, G, P])
        sq = sb("sq", [P, G * 2 * HEADS, HD])
        n2 = sb("n2", [P, G * 2 * HEADS])
        nrm = sb("nrm", [P, G * 2 * HEADS])
        rn = sb("rn", [P, G * 2 * HEADS])
        qk = sb("qk", [P, 2, G, 2 * D])
        qT = sb("qT", [P, G, P])
        xk = sb("xk", [P, BG * D])
        mt = sb("mt", [P, BG * D])
        gm = sb("gm", [P, BG * D])
        stats2 = sb("stats2", [P, G, 6])
        sv2 = sb("sv2", [P, G, 2])
        md2 = sb("md2", [P, G])
        var2 = sb("var2", [P, G])
        std2 = sb("std2", [P, G])
        rstd2 = sb("rstd2", [P, G])
        mms2 = sb("mms2", [P, G])
        row = sb("row", [P, 2, G, K, ROW])
        x2T = sb("x2T", [P, G, P])
        logit = sb("logit", [P, NT, E])
        top = sb("top", [P, K, NT])
        eq = sb("eq", [P, G, E])
        key = sb("key", [P, G, E])
        kmax = sb("kmax", [P, G])
        sel = sb("sel", [P, G, K, E])
        rest = sb("rest", [P, G, E])
        mask = sb("mask", [P, G, E], BF16)
        msum = sb("msum", [P, E])
        seen = sb("seen", [P, E], BF16)
        pos = sb("pos", [P, G, E])
        spos = sb("spos", [P, G, K, E])
        slot = sb("slot", [P, 2, G, K], I32)
        cnt = sb("cnt", [1, E])
        cnti = sb("cnti", [1, E], I32)
        tilesi = sb("tilesi", [1, E], I32)
        tiles = sb("tiles", [1, E])
        tend = sb("tend", [1, E])
        tinc = sb("tinc", [1, E])
        past = sb("past", [1, NS, E])
        pinc = sb("pinc", [1, NS, E])
        esum = sb("esum", [1, NS])
        rsum = sb("rsum", [1, NS])
        etab = sb("etab", [1, NS], I32)
        rtab = sb("rtab", [1, NS], I32)
        ptab = sb("ptab", [1, E], I32)
        onee = sb("onee", [1, E])
        scratch = sb("scratch", [1, 2])
        dlog = sb("dlog", [P, NT, E])
        elog = sb("elog", [P, NT, E])
        dtop = sb("dtop", [P, NT])
        etop = sb("etop", [P, NT])
        esm = sb("esm", [P, NT])
        gate = sb("gate", [P, K, NT])
        xt = sb("xt", [P, U, ROW])
        xT = sb("xT", [P, 2, P])
        h = sb("h", [P, 2, F])
        hT = sb("hT", [P, 2, FC, P])
        y = sb("y", [P, U, D])
        yback = sb("yback", [P, 2, K, G, D])

        psX = pb("psX", [P, 512])
        psQK = pb("psQK", [P, 1024])
        psQ = pb("psQ", [P, 512])
        psKV = pb("psKV", [P, 512])
        psG = pb("psG", [P, 512])
        psO = pb("psO", [P, 512])
        psW = pb("psW", [P, 512])
        psXK, psMT = psKV[:, 0:BG * D], psKV[:, BG * D:2 * BG * D]
        psGM = psG[:, 0:BG * D]
        psL = psG[:, 256:256 + G * E].rearrange("p (g e) -> p g e", g=G)
        psPos = psG[:, 320:320 + G * E].rearrange("p (g e) -> p g e", g=G)
        psCnt = psG[0:1, 384:384 + E]
        psXT = [psX[:, 0:P], psW[:, 0:P]]
        psH = [psQK[:, 0:F], psQK[:, 512:512 + F]]
        psHT = [psQ, psKV]
        psY = [psO[:, 0:D], psG[:, 0:D]]

        s_xin = [sem(f"s_xin{i}") for i in range(3)]
        s_wa = sem("s_wa")
        s_wb = sem("s_wb")
        s_w2 = sem("s_w2")
        s_zero = sem("s_zero")
        s_const = sem("s_const")
        s_iota = sem("s_iota")
        s_cf = sem("s_cf")
        s_ea = sem("s_ea")
        s_eb = sem("s_eb")
        s_hm = sem("s_hm")
        s_pw = sem("s_pw")
        s_w = sem("s_w")
        s_wg = sem("s_wg")
        s_bo = sem("s_bo")
        s_st = sem("s_st")
        s_hf = sem("s_hf")
        s_hf2 = sem("s_hf2")
        s_mv = sem("s_mv")
        s_std = sem("s_std")
        s_rstd = sem("s_rstd")
        s_xn = sem("s_xn")
        s_psX = sem("s_psX")
        s_xnT = sem("s_xnT")
        s_psQK = sem("s_psQK")
        s_sq = sem("s_sq")
        s_n2r = sem("s_n2r")
        s_n2 = sem("s_n2")
        s_nrm = sem("s_nrm")
        s_rn = sem("s_rn")
        s_qk = sem("s_qk")
        s_psQ = sem("s_psQ")
        s_psXK = sem("s_psXK")
        s_qT = sem("s_qT")
        s_xk = sem("s_xk")
        s_psMT = sem("s_psMT")
        s_mt = sem("s_mt")
        s_psGM = sem("s_psGM")
        s_gm = sem("s_gm")
        s_psO = sem("s_psO")
        s_x2 = sem("s_x2")
        s_st2 = sem("s_st2")
        s_mv2 = sem("s_mv2")
        s_std2 = sem("s_std2")
        s_rstd2 = sem("s_rstd2")
        s_row = sem("s_row")
        s_psR = sem("s_psR")
        s_x2T = sem("s_x2T")
        s_psW = sem("s_psW")
        s_w1 = sem("s_w1")
        s_psL = sem("s_psL")
        s_xb = sem("s_xb")
        s_rt = sem("s_rt")
        s_sp = sem("s_sp")
        s_carry = sem("s_carry")
        s_mask = sem("s_mask")
        s_psPos = sem("s_psPos")
        s_seen = sem("s_seen")
        s_pos = sem("s_pos")
        s_slot = sem("s_slot")
        s_scat = [sem(f"s_scat{i}") for i in range(2)]
        s_cnt = sem("s_cnt")
        s_tb = sem("s_tb")
        s_tab = sem("s_tab")
        s_pad = sem("s_pad")
        s_dlog = sem("s_dlog")
        s_elog = sem("s_elog")
        s_gt = sem("s_gt")
        s_gate = sem("s_gate")
        s_xt = [sem(f"s_xt{i}") for i in range(U)]
        s_psXT = sem("s_psXT")
        s_xT = sem("s_xT")
        s_psH = sem("s_psH")
        s_h = sem("s_h")
        s_psHT = sem("s_psHT")
        s_hT = sem("s_hT")
        s_psY = sem("s_psY")
        s_y = sem("s_y")
        s_back = [sem(f"s_back{i}") for i in range(U)]
        s_yb = [sem(f"s_yb{i}") for i in range(2)]
        s_o1 = sem("s_o1")
        s_o = sem("s_o")
        s_out = sem("s_out")

        block = ctx.enter_context(nc.Block())

        def after(eng, s, v):
            if not isinstance(v, int) or v > 0:
                eng.wait_ge(s, v)

        def run_groups(eng, slot_of):
            slot_of(0, None, None, None)
            slot_of(1, 0, 0, 0)
            slot_of(2, 1, 1, 0)
            with eng.Fori(1, NG // 2 - 1) as i:
                slot_of(i * 2 + 1, i * 2, 0, i)
                slot_of(i * 2 + 2, i * 2 + 1, 1, i)
            slot_of(NG - 1, NG - 2, 0, NG // 2 - 1)
            slot_of(None, NG - 1, 1, NG // 2 - 1)

        def run_slots(eng, one):
            for b in range(U):
                one(b, b, 0)
            with eng.Fori(1, NS // U - 1) as i:
                for b in range(U):
                    one(i * U + b, b, i)
            for b in range(U):
                one(NS - U + b, b, NS // U - 1)

        def tiles_of(t, g):
            return t[:, bass.ds(g * G, G)]

        @block.sync
        def _(sp):
            sp.dma_start(xin[:, 0:G, :], x_v[:, 0:G, :]).then_inc(s_xin[0], 16)
            sp.dma_start(wqk[:, 0:D], Wq).then_inc(s_wa, 16)
            sp.dma_start(wqk[:, D:2 * D], Wk).then_inc(s_wa, 16)
            sp.dma_start(wv[:], Wv).then_inc(s_wa, 16)
            sp.dma_start(wo[:], Wo).then_inc(s_wa, 16)
            sp.dma_start(wgrow[:], Wg).then_inc(s_wa, 16)
            sp.dma_start(xin[:, G:2 * G, :], x_v[:, G:2 * G, :]).then_inc(s_xin[1], 16)
            sp.dma_start(xin[:, 2 * G:NT, :], x_v[:, 2 * G:NT, :]).then_inc(s_xin[2], 16)
            sp.dma_start(b1row[:], b1.rearrange("e f -> (e f)").rearrange("(a e f) -> a e f", a=1, e=E)).then_inc(s_wb, 16)
            sp.dma_start(w1s[:], w1.rearrange("e d f -> d e f")).then_inc(s_wb, 16)
            sp.dma_start(w2s[:], w2.rearrange("e (c p) d -> p e c d", p=P)).then_inc(s_w2, 16)
            sp.dma_start(b2bc[:], b2.partition_broadcast(P)).then_inc(s_w2, 16)
            sp.wait_ge(s_zero, 2)
            sp.dma_start(xs[E * REGION:E * REGION + P, :], padrow[:]).then_inc(s_pad, 16)
            sp.wait_ge(s_tab, 1)
            with sp.Fori(0, E) as e:
                r = sp.value_load(ptab[0:1, bass.ds(e, 1)], min_val=0, max_val=E * REGION - P)
                sp.dma_start(xs[bass.ds(r, P), :], padrow[:]).then_inc(s_pad, 16)
            sp.wait_ge(s_pad, 16 * (E + 1))
            for p in range(2):
                sp.wait_ge(s_scat[p], 16 * G * K * NG // 2)

            def load(s, b, i):
                after(sp, s_back[b], 16 * i)
                r = sp.value_load(rtab[0:1, bass.ds(s, 1)], min_val=0, max_val=E * REGION)
                sp.dma_start(xt[:, b, :], xs[bass.ds(r, P), :]).then_inc(s_xt[b], 16)
            run_slots(sp, load)

            for b in range(U):
                sp.wait_ge(s_back[b], 16 * (NS // U))
            for c in range(2):
                for k in range(K):
                    sp.dma_start(yback[:, c, k], ys_v[:, k, c * G:(c + 1) * G, :]).then_inc(s_yb[c], 16)

            def give(c, p, more):
                sp.wait_ge(s_o, c + 1)
                sp.dma_start(out_v[:, bass.ds(c * G, G), :], tiles_of(x2, c)).then_inc(s_out, 16)
                if more:
                    for k in range(K):
                        sp.dma_start(yback[:, p, k], ys_v[:, k, bass.ds(c * G + 2 * G, G), :]).then_inc(s_yb[p], 16)
            with sp.Fori(0, NG // 2 - 1) as i:
                give(i * 2, 0, True)
                give(i * 2 + 1, 1, True)
            give(NG - 2, 0, False)
            give(NG - 1, 1, False)
            sp.wait_ge(s_out, 16 * NG)

        @block.gpsimd
        def _(pool):
            pool.memset(ident[:], 0.0)
            pool.memset(headmask[:], 1.0)
            pool.memset(tri[:], 1.0)
            pool.memset(padrow[:], 0.0)
            pool.memset(ones[:], 1.0)
            pool.memset(negmean[:], -1.0 / D)
            pool.memset(onerow[:], 1.0 / D)
            pool.memset(eps[:], LN_EPS)
            pool.memset(onee[:], 1.0)
            pool.memset(scratch[:], 0.0)
            pool.memset(seen[:], 0.0).then_inc(s_zero, 1)
            pool.wait_ge(s_zero, 1)
            pool.affine_select(out=ident[:], in_=ident[:], compare_op=ALU.not_equal, fill=1.0, base=0,
                               pattern=[[-1, P]], channel_multiplier=1)
            pool.affine_select(out=tri[:], in_=tri[:], compare_op=ALU.is_ge, fill=0.0, base=-1,
                               pattern=[[1, P]], channel_multiplier=-1)
            hm = headmask[:].rearrange("p (h d) -> p h d", h=HEADS)
            pool.affine_select(out=hm, in_=hm, compare_op=ALU.is_ge, fill=0.0, base=0,
                               pattern=[[-HD, HEADS], [0, HD]], channel_multiplier=1).then_inc(s_const, 1)
            pool.wait_ge(s_const, 1)
            pool.affine_select(out=hm, in_=hm, compare_op=ALU.is_ge, fill=0.0, base=HD - 1,
                               pattern=[[HD, HEADS], [0, HD]], channel_multiplier=-1).then_inc(s_const, 1)
            pool.iota(padrow[:, D:ROW].bitcast(I32), pattern=[[0, 1]], base=SENT_OUT,
                      channel_multiplier=0).then_inc(s_zero, 1)
            pool.iota(revi[:], pattern=[[0, G], [-1, E]], base=E, channel_multiplier=0)
            pool.iota(regbasei[:], pattern=[[0, G], [REGION, E]], base=0, channel_multiplier=0)
            pool.iota(dest[:], pattern=[[P, NT], [T, K]], base=0, channel_multiplier=1)
            pool.iota(sidxi[:], pattern=[[1, NS]], base=0, channel_multiplier=0).then_inc(s_iota, 1)

            xs_bound = pool.to_reg(E * REGION - 1)
            ys_bound = pool.to_reg(K * T - 1)

            def carry_wait(n):
                after(pool, s_carry, n)
                pool.tensor_tensor(scratch[0:1, 1:2], scratch[0:1, 0:1], scratch[0:1, 0:1], ALU.add).then_inc(s_carry, 1)

            def slot_of(ga, gb, p, i):
                if ga is not None:
                    for c in range(3):
                        if isinstance(ga, int) and ga == c:
                            pool.wait_ge(s_xin[c], 16)
                    if not isinstance(ga, int):
                        pool.wait_ge(s_xin[2], 16)
                    if isinstance(ga, int) and ga == 0:
                        pool.wait_ge(s_bo, 16)
                    pool.tensor_tensor(tiles_of(x2, ga), tiles_of(xin, ga),
                                       bobc[:].unsqueeze(1).to_broadcast([P, G, D]), ALU.add).then_inc(s_xb, 1)
                if gb is not None:
                    pool.wait_ge(s_slot, gb + 1)
                    carry_wait(gb)
                    for j in range(G):
                        for k in range(K):
                            pool.indirect_dma_start(
                                out=xs, out_offset=bass.IndirectOffsetOnAxis(ap=slot[:, p, j, k:k + 1], axis=0),
                                in_=row[:, p, j, k, :], in_offset=None,
                                bounds_check=xs_bound, oob_is_err=False).then_inc(s_scat[p], 16)
            run_groups(pool, slot_of)

            def put(s, b, i):
                pool.wait_ge(s_y, s + 1)
                carry_wait(s + NG)
                pool.indirect_dma_start(
                    out=ys, out_offset=bass.IndirectOffsetOnAxis(ap=xt[:, b, D:ROW].bitcast(I32), axis=0),
                    in_=y[:, b, :], in_offset=None,
                    bounds_check=ys_bound, oob_is_err=False).then_inc(s_back[b], 16)
            run_slots(pool, put)

        @block.tensor
        def _(pe):
            def centred(dst, src, bias):
                mm = pe.matmul(dst, negmean[:], src, start=True, stop=bias is None)
                if bias is not None:
                    mm = pe.matmul(dst, onerow[:], bias, start=False, stop=True)
                return mm

            pe.wait_ge(s_zero, 2)
            pe.wait_ge(s_const, 2)
            pe.wait_ge(s_wa, 16 * 5)
            pe.wait_ge(s_ea, 16 * 3)
            pe.transpose(psW[:, 0:E], wgrow[:], ident[0:E, 0:E]).then_inc(s_pw, 1)
            centred(psQK[:, 0:2 * D], wqk[:], brow[0:1, 0:2 * D])
            centred(psO[:, 0:D], wv[:], brow[0:1, 2 * D:3 * D]).then_inc(s_pw, 1)
            pe.wait_ge(s_wg, 1)
            centred(psG[:, 0:E], wgT[:], None).then_inc(s_pw, 1)

            def slot_of(ga, gb, p, i):
                pa = 0 if gb is None else 1 - p if ga is not None else None
                if gb is not None:
                    pe.wait_ge(s_qk, gb + 1)
                    after(pe, s_x2T, gb)
                    for j in range(G):
                        mm = pe.transpose(psQ[:, j * P:(j + 1) * P], qk[:, p, j, 0:D], ident[:])
                    mm.then_inc(s_psQ, 1)
                    after(pe, s_mt, gb)
                    for b in range(BG):
                        for u in range(TB):
                            mm = pe.matmul(psXK[:, b * D:(b + 1) * D], xn[:, p, b * TB + u, :],
                                           qk[:, p, b * TB + u, D:2 * D], start=u == 0, stop=u == TB - 1)
                    mm.then_inc(s_psXK, 1)
                    pe.wait_ge(s_xk, gb + 1)
                    if isinstance(gb, int) and gb == 0:
                        pe.wait_ge(s_w, 2)
                    pe.matmul(psMT, wv[:], xk[:], start=True, stop=True).then_inc(s_psMT, 1)
                if ga is not None:
                    pe.wait_ge(s_xn, ga + 1)
                    after(pe, s_xnT, ga)
                    for j in range(G):
                        mm = pe.transpose(psX[:, j * P:(j + 1) * P], xn[:, pa, j, :], ident[:])
                    mm.then_inc(s_psX, 1)
                if gb is not None:
                    pe.wait_ge(s_mt, gb + 1)
                    after(pe, s_pos, gb)
                    for b in range(BG):
                        mm = pe.matmul(psGM[:, b * D:(b + 1) * D], mt[:, b * D:(b + 1) * D], wo[:],
                                       start=True, stop=True)
                    mm.then_inc(s_psGM, 1)
                if ga is not None:
                    pe.wait_ge(s_xnT, ga + 1)
                    if isinstance(ga, int) and ga == 0:
                        pe.wait_ge(s_w, 2)
                    after(pe, s_qk, ga)
                    for j in range(G):
                        mm = pe.matmul(psQK[:, j * 2 * D:(j + 1) * 2 * D], xnT[:, j, :], wqk[:], start=True, stop=True)
                    mm.then_inc(s_psQK, 1)
                if gb is not None:
                    pe.wait_ge(s_qT, gb + 1)
                    pe.wait_ge(s_gm, gb + 1)
                    after(pe, s_x2, gb)
                    for j in range(G):
                        mm = pe.matmul(psO[:, j * D:(j + 1) * D], qT[:, j, :], gm[:, j // TB * D:(j // TB + 1) * D],
                                       start=True, stop=True)
                    mm.then_inc(s_psO, 1)
                    if isinstance(gb, int) and gb == 0:
                        pe.wait_ge(s_wb, 32)
                        pe.wait_ge(s_w, 3)
                    after(pe, s_w1, gb)
                    centred(psW[:], w1s[:, bass.ds(gb, 1), :], b1row[0:1, bass.ds(gb, 1), :]).then_inc(s_psW, 1)
                    pe.wait_ge(s_row, gb + 1)
                    for j in range(G):
                        mm = pe.transpose(psQ[:, j * P:(j + 1) * P], row[:, p, j, 0, 0:D], ident[:])
                    mm.then_inc(s_psR, 1)
                    pe.wait_ge(s_x2T, gb + 1)
                    for j in range(G):
                        mm = pe.matmul(psL[:, j, :], x2T[:, j, :], wgT[:], start=True, stop=True)
                    mm.then_inc(s_psL, 1)
                    pe.wait_ge(s_mask, gb + 1)
                    pe.matmul(psPos, tri[:], mask[:], start=True, stop=False)
                    for j in range(G - 1):
                        pe.matmul(psPos[:, j + 1:G, :], ones[:], mask[:, j:j + 1, :].to_broadcast([P, G - 1 - j, E]),
                                  start=False, stop=False)
                    pe.matmul(psPos, ones[:], seen[:].unsqueeze(1).to_broadcast([P, G, E]),
                              start=False, stop=True).then_inc(s_psPos, 1)
            run_groups(pe, slot_of)

            pe.wait_ge(s_seen, NG)
            pe.matmul(psCnt, ones[:, 0:1], seen[:], start=True, stop=True).then_inc(s_cnt, 1)

            pe.wait_ge(s_tab, 1)
            pe.wait_ge(s_w1, E)
            pe.wait_ge(s_w2, 32)

            def expert(s):
                return pe.value_load(etab[0:1, bass.ds(s, 1)], min_val=0, max_val=E - 1)

            def turn_in(s, b, i):
                q = b % 2
                pe.wait_ge(s_xt[b], (i + 1) * 16)
                after(pe, s_xT, s - 1)
                pe.transpose(psXT[q], xt[:, b, 0:D], ident[:]).then_inc(s_psXT, 1)

            def up(s, b):
                q = b % 2
                e = expert(s)
                pe.wait_ge(s_xT, s + 1)
                after(pe, s_h, s - 1)
                pe.matmul(psH[q], xT[:, q, :], w1s[:, bass.ds(e, 1), :], start=True, stop=True).then_inc(s_psH, 1)

            def turn_h(s, b):
                q = b % 2
                pe.wait_ge(s_h, s + 1)
                after(pe, s_hT, s - 1)
                for c in range(FC):
                    mm = pe.transpose(psHT[q][:, c * P:(c + 1) * P], h[:, q, c * P:(c + 1) * P], ident[:])
                mm.then_inc(s_psHT, 1)

            def down(s, b):
                q = b % 2
                e = expert(s)
                pe.wait_ge(s_hT, s + 1)
                after(pe, s_y, s - 1)
                for c in range(FC):
                    mm = pe.matmul(psY[q], hT[:, q, c, :], w2s[:, bass.ds(e, 1), c, :],
                                   start=c == 0, stop=c == FC - 1)
                mm.then_inc(s_psY, 1)

            turn_in(0, 0, 0)
            turn_in(1, 1, 0)
            up(0, 0)

            def one(s, b, i):
                last = isinstance(s, int)
                if not (last and s + 2 >= NS):
                    turn_in(s + 2, (b + 2) % U, i + (b + 2) // U)
                if not (last and s + 1 >= NS):
                    up(s + 1, (b + 1) % U)
                turn_h(s, b)
                if not (last and s == 0):
                    down(s - 1, (b - 1) % U)
            run_slots(pe, one)
            down(NS - 1, U - 1)

        @block.scalar
        def _(act):
            act.dma_start(brow[0:1, 0:D], bq.rearrange("(a f) -> a f", a=1)).then_inc(s_ea, 16)
            act.dma_start(brow[0:1, D:2 * D], bk.rearrange("(a f) -> a f", a=1)).then_inc(s_ea, 16)
            act.dma_start(brow[0:1, 2 * D:3 * D], bv.rearrange("(a f) -> a f", a=1)).then_inc(s_ea, 16)
            act.dma_start(bobc[:], bo.partition_broadcast(P)).then_inc(s_bo, 16)
            act.dma_start(mcol[:], m.rearrange("(h a) -> h a", a=1).to_broadcast([HEADS, HD])).then_inc(s_hm, 16)
            act.wait_ge(s_hm, 16)
            act.activation(mcol[:], mcol[:], ACT.Exp, scale=-1.0).then_inc(s_eb, 1)
            act.wait_ge(s_eb, 3)
            act.activation(mcol[:], mcol[:], ACT.Exp, scale=-float(np.log(S))).then_inc(s_eb, 1)

            def slot_of(ga, gb, p, i):
                if ga is not None:
                    act.wait_ge(s_mv, ga + 1)
                    act.activation(std[:], var[:], ACT.Sqrt, bias=eps[:, 0:1], scale=1.0 / D).then_inc(s_std, 1)
                if gb is not None:
                    act.wait_ge(s_psQ, gb + 1)
                    act.copy(qT[:], psQ[:].rearrange("p (g t) -> p g t", g=G)).then_inc(s_qT, 1)
                if ga is not None:
                    act.wait_ge(s_psX, ga + 1)
                    act.copy(xnT[:], psX[:].rearrange("p (g t) -> p g t", g=G)).then_inc(s_xnT, 1)
                if gb is not None:
                    act.wait_ge(s_psGM, gb + 1)
                    act.copy(gm[:], psGM).then_inc(s_gm, 1)
                if ga is not None:
                    act.wait_ge(s_psQK, ga + 1)
                    after(act, s_n2, ga)
                    act.activation(sq[:].rearrange("p a d -> p (a d)"), psQK[:], ACT.Square).then_inc(s_sq, 1)
                if gb is not None:
                    act.wait_ge(s_mv2, gb + 1)
                    act.activation(std2[:], var2[:], ACT.Sqrt, bias=eps[:, 0:1], scale=1.0 / D).then_inc(s_std2, 1)
                if ga is not None:
                    act.wait_ge(s_n2, ga + 1)
                    act.activation(nrm[:], n2[:], ACT.Sqrt).then_inc(s_nrm, 1)
                if gb is not None:
                    act.wait_ge(s_psR, gb + 1)
                    act.copy(x2T[:], psQ[:].rearrange("p (g t) -> p g t", g=G)).then_inc(s_x2T, 1)
            run_groups(act, slot_of)

            act.wait_ge(s_dlog, 1)
            act.activation(elog[:], dlog[:], ACT.Exp)
            act.activation(etop[:], dtop[:], ACT.Exp).then_inc(s_elog, 1)

            def xin_T(s, b):
                act.wait_ge(s_psXT, s + 1)
                after(act, s_psH, s - 1)
                act.copy(xT[:, b % 2, :], psXT[b % 2]).then_inc(s_xT, 1)

            def one(s, b, i):
                if not (isinstance(s, int) and s + 1 >= NS):
                    xin_T(s + 1, b + 1)
                act.wait_ge(s_psH, s + 1)
                after(act, s_psHT, s - 1)
                act.activation(h[:, b % 2, :], psH[b % 2], ACT.Gelu).then_inc(s_h, 1)
            xin_T(0, 0)
            run_slots(act, one)

        @block.vector
        def _(dve):
            dve.wait_ge(s_iota, 1)
            dve.tensor_copy(rev[:], revi[:])
            dve.tensor_copy(regbase[:], regbasei[:])
            dve.tensor_copy(sidx[:], sidxi[:]).then_inc(s_cf, 1)

            def weights():
                dve.wait_ge(s_pw, 1)
                dve.tensor_copy(wgT[:], psW[:, 0:E]).then_inc(s_wg, 1)
                dve.wait_ge(s_pw, 2)
                dve.tensor_tensor(wqk[:], psQK[:, 0:2 * D], wqk[:], ALU.add).then_inc(s_w, 1)
                dve.tensor_tensor(wv[:], psO[:, 0:D], wv[:], ALU.add).then_inc(s_w, 1)
                dve.wait_ge(s_pw, 3)
                dve.tensor_tensor(wgT[:], psG[:, 0:E], wgT[:], ALU.add).then_inc(s_w, 1)
                dve.wait_ge(s_eb, 1)
                dve.tensor_scalar(mcol[:], mcol[:], 1.0, None, ALU.add).then_inc(s_eb, 1)
                dve.wait_ge(s_eb, 2)
                dve.reciprocal(mcol[:], mcol[:]).then_inc(s_eb, 1)
                dve.wait_ge(s_eb, 4)
                dve.wait_ge(s_const, 2)
                dve.tensor_scalar(headmask[:], headmask[:], mcol[:, 0:1], None, ALU.mult).then_inc(s_cf, 1)

            def halves(src, g, st, s_stats):
                for j in range(G):
                    b = dve.bn_stats(st[:, j, :], tiles_of(src, g)[:, j, :])
                b.then_inc(s_stats, 1)

            def moments(st, sv, md, var, s_stats, s_half, s_done, n):
                dve.wait_ge(s_stats, n)
                dve.tensor_tensor(sv[:], st[:, :, 1:3], st[:, :, 4:6], ALU.add)
                dve.tensor_tensor(md[:], st[:, :, 1], st[:, :, 4], ALU.subtract).then_inc(s_half, 1)
                dve.wait_ge(s_half, 2 * n - 1)
                dve.tensor_tensor(md[:], md[:], md[:], ALU.mult).then_inc(s_half, 1)
                dve.wait_ge(s_half, 2 * n)
                dve.scalar_tensor_tensor(out=var[:], in0=md[:], scalar=D / 4.0, in1=sv[:, :, 1],
                                         op0=ALU.mult, op1=ALU.add).then_inc(s_done, 1)

            def centre(mms, rstd, sv, std, s_done):
                dve.reciprocal(rstd[:], std[:])
                dve.scalar_tensor_tensor(out=mms[:], in0=sv[:, :, 0], scalar=0.5, in1=std[:],
                                         op0=ALU.mult, op1=ALU.subtract).then_inc(s_done, 1)

            def first_argmax(values, gb, k, waits):
                r0 = waits
                best = top[:, k, bass.ds(gb * G, G)]
                dve.tensor_reduce(best, values, AX, ALU.max).then_inc(s_rt, 1)
                dve.wait_ge(s_rt, r0 + 1)
                dve.tensor_tensor(eq[:], values, best.unsqueeze(2).to_broadcast([P, G, E]),
                                  ALU.is_equal).then_inc(s_rt, 1)
                dve.wait_ge(s_rt, r0 + 2)
                dve.tensor_tensor(key[:], eq[:], rev[:], ALU.mult).then_inc(s_rt, 1)
                dve.wait_ge(s_rt, r0 + 3)
                dve.tensor_reduce(kmax[:], key[:], AX, ALU.max).then_inc(s_rt, 1)
                dve.wait_ge(s_rt, r0 + 4)
                dve.tensor_tensor(sel[:, :, k, :], key[:], kmax[:].unsqueeze(2).to_broadcast([P, G, E]),
                                  ALU.is_equal).then_inc(s_rt, 1)
                dve.wait_ge(s_rt, r0 + 5)

            def slot_of(ga, gb, p, i):
                pa = 0 if gb is None else 1 - p if ga is not None else None
                if ga is not None:
                    if isinstance(ga, int):
                        dve.wait_ge(s_xin[min(ga, 2)], 16)
                    else:
                        dve.wait_ge(s_xin[2], 16)
                    halves(xin, ga, stats, s_st)
                    moments(stats, sv, md, var, s_st, s_hf, s_mv, ga + 1)
                if isinstance(ga, int) and ga == 0:
                    weights()
                if gb is not None:
                    dve.wait_ge(s_psXK, gb + 1)
                    dve.tensor_copy(xk[:], psXK).then_inc(s_xk, 1)
                if ga is not None:
                    dve.wait_ge(s_std, ga + 1)
                    centre(mms, rstd, sv, std, s_rstd)
                    dve.wait_ge(s_rstd, ga + 1)
                    for j in range(G):
                        b = dve.tensor_scalar(xn[:, pa, j, :], tiles_of(xin, ga)[:, j, :], mms[:, j:j + 1],
                                              rstd[:, j:j + 1], ALU.subtract, ALU.mult)
                    b.then_inc(s_xn, 1)
                if gb is not None:
                    dve.wait_ge(s_psMT, gb + 1)
                    if isinstance(gb, int) and gb == 0:
                        dve.wait_ge(s_cf, 2)
                    dve.tensor_tensor(mt[:].rearrange("p (b f) -> p b f", b=BG),
                                      psMT.rearrange("p (b f) -> p b f", b=BG),
                                      headmask[:].unsqueeze(1).to_broadcast([P, BG, D]), ALU.mult).then_inc(s_mt, 1)
                    dve.wait_ge(s_psO, gb + 1)
                    dve.wait_ge(s_xb, gb + 1)
                    dve.tensor_tensor(tiles_of(x2, gb), psO[:].rearrange("p (g f) -> p g f", g=G),
                                      tiles_of(x2, gb), ALU.add).then_inc(s_x2, 1)
                if ga is not None:
                    if gb is not None:
                        dve.wait_ge(s_x2, gb + 1)
                    dve.wait_ge(s_sq, ga + 1)
                    dve.tensor_reduce(n2[:], sq[:], AX, ALU.add).then_inc(s_n2r, 1)
                if gb is not None:
                    dve.wait_ge(s_x2, NG) if ga is None else None
                    halves(x2, gb, stats2, s_st2)
                    moments(stats2, sv2, md2, var2, s_st2, s_hf2, s_mv2, gb + 1)
                if ga is not None:
                    dve.wait_ge(s_n2r, ga + 1)
                    dve.tensor_scalar(n2[:], n2[:], L2_EPS * L2_EPS, None, ALU.max).then_inc(s_n2, 1)
                if gb is not None:
                    dve.wait_ge(s_std2, gb + 1)
                    centre(mms2, rstd2, sv2, std2, s_rstd2)
                    dve.wait_ge(s_rstd2, gb + 1)
                    after(dve, s_scat[p], i * 16 * G * K)
                    for j in range(G):
                        dve.tensor_scalar(row[:, p, j, :, 0:D],
                                          tiles_of(x2, gb)[:, j:j + 1, :].to_broadcast([P, K, D]),
                                          mms2[:, j:j + 1], rstd2[:, j:j + 1], ALU.subtract, ALU.mult)
                    dve.tensor_copy(row[:, p, :, :, D:ROW].bitcast(I32).rearrange("p g k a -> p g (k a)"),
                                    dest[:, bass.ds(gb * G, G), :]).then_inc(s_row, 1)
                if ga is not None:
                    dve.wait_ge(s_nrm, ga + 1)
                    dve.reciprocal(rn[:], nrm[:]).then_inc(s_rn, 1)
                    dve.wait_ge(s_rn, ga + 1)
                    dve.tensor_tensor(qk[:, pa].rearrange("p g (h d) -> p (g h) d", d=HD),
                                      psQK[:].rearrange("p (a d) -> p a d", d=HD),
                                      rn[:].unsqueeze(2).to_broadcast([P, G * 2 * HEADS, HD]), ALU.mult).then_inc(s_qk, 1)
                if gb is not None:
                    dve.wait_ge(s_psW, gb + 1)
                    w = w1s[:, bass.ds(gb, 1), :]
                    dve.tensor_tensor(w, psW[:].unsqueeze(1), w, ALU.add).then_inc(s_w1, 1)
                    dve.wait_ge(s_psL, gb + 1)
                    lg = tiles_of(logit, gb)
                    dve.tensor_copy(lg, psL).then_inc(s_rt, 1)
                    r = gb * 13
                    dve.wait_ge(s_rt, r + 1)
                    first_argmax(lg, gb, 0, r + 1)
                    dve.scalar_tensor_tensor(out=rest[:], in0=sel[:, :, 0, :], scalar=-3e38, in1=lg,
                                             op0=ALU.mult, op1=ALU.add).then_inc(s_rt, 1)
                    dve.wait_ge(s_rt, r + 7)
                    first_argmax(rest[:], gb, 1, r + 7)
                    after(dve, s_psPos, gb)
                    dve.tensor_tensor(mask[:], sel[:, :, 0, :], sel[:, :, 1, :], ALU.add).then_inc(s_mask, 1)
                    dve.wait_ge(s_mask, gb + 1)
                    dve.tensor_reduce(msum[:], mask[:].rearrange("p g e -> p e g"), AX, ALU.add).then_inc(s_rt, 1)
                    dve.wait_ge(s_psPos, gb + 1)
                    dve.tensor_tensor(pos[:], psPos, regbase[:], ALU.add).then_inc(s_pos, 1)
                    dve.wait_ge(s_rt, r + 13)
                    dve.tensor_tensor(seen[:], seen[:], msum[:], ALU.add).then_inc(s_seen, 1)
                    dve.wait_ge(s_pos, gb + 1)
                    for k in range(K):
                        b = dve.tensor_tensor(spos[:, :, k, :], sel[:, :, k, :], pos[:], ALU.mult)
                    b.then_inc(s_sp, 1)
                    dve.wait_ge(s_sp, gb + 1)
                    with nc.allow_low_precision(reason="row numbers below 2**24, summed in float32"):
                        dve.tensor_reduce(slot[:, p], spos[:], AX, ALU.add).then_inc(s_slot, 1)
            run_groups(dve, slot_of)

            n = 0

            def chain(ins):
                nonlocal n
                n += 1
                ins.then_inc(s_tb, 1)
                dve.wait_ge(s_tb, n)
            dve.wait_ge(s_cnt, 1)
            chain(dve.tensor_copy(cnt[:], psCnt))
            dve.tensor_tensor(ptab[:], cnt[:], regbase[0:1, 0, :], ALU.add)
            chain(dve.tensor_scalar(cnti[:], cnt[:], float(P - 1), None, ALU.add))
            chain(dve.tensor_scalar(tilesi[:], cnti[:], P.bit_length() - 1, None, ALU.logical_shift_right))
            chain(dve.tensor_copy(tiles[:], tilesi[:]))
            dve.tensor_tensor_scan(tend[:], onee[:], tiles[:], 0.0, ALU.mult, ALU.add)
            chain(dve.tensor_scalar(tinc[:], tiles[:], -float(P), float(REGION), ALU.mult, ALU.add))
            chain(dve.tensor_tensor(past[:], sidx[:].unsqueeze(2).to_broadcast([1, NS, E]),
                                    tend[:].unsqueeze(1).to_broadcast([1, NS, E]), ALU.is_ge))
            dve.tensor_reduce(esum[:], past[:], AX, ALU.add)
            chain(dve.tensor_tensor(pinc[:], past[:], tinc[:].unsqueeze(1).to_broadcast([1, NS, E]), ALU.mult))
            dve.tensor_scalar(etab[:], esum[:], float(E - 1), None, ALU.min)
            chain(dve.tensor_reduce(rsum[:], pinc[:], AX, ALU.add))
            chain(dve.scalar_tensor_tensor(out=rsum[:], in0=sidx[:], scalar=float(P), in1=rsum[:],
                                           op0=ALU.mult, op1=ALU.add))
            dve.tensor_scalar(rtab[:], rsum[:], float(E * REGION), None, ALU.min).then_inc(s_tab, 1)
            dve.tensor_tensor(dtop[:], top[:, 1, :], top[:, 0, :], ALU.subtract)
            dve.tensor_tensor(dlog[:], logit[:], top[:, 0, :].unsqueeze(2).to_broadcast([P, NT, E]),
                              ALU.subtract).then_inc(s_dlog, 1)
            dve.wait_ge(s_elog, 1)
            dve.tensor_reduce(esm[:], elog[:], AX, ALU.add).then_inc(s_gt, 1)
            dve.wait_ge(s_gt, 1)
            dve.reciprocal(gate[:, 0, :], esm[:]).then_inc(s_gt, 1)
            dve.wait_ge(s_gt, 2)
            dve.tensor_tensor(gate[:, 1, :], etop[:], gate[:, 0, :], ALU.mult).then_inc(s_gate, 1)

            def turned(s, b):
                dve.wait_ge(s_psHT, s + 1)
                after(dve, s_psY, s - 1)
                dve.tensor_copy(hT[:, b % 2], psHT[b % 2][:].rearrange("p (c t) -> p c t", c=FC)).then_inc(s_hT, 1)

            def result(s, b, i):
                e = dve.value_load(etab[0:1, bass.ds(s, 1)], min_val=0, max_val=E - 1)
                dve.wait_ge(s_psY, s + 1)
                after(dve, s_back[b], 16 * i)
                dve.tensor_tensor(y[:, b:b + 1, :], psY[b % 2].unsqueeze(1), b2bc[:, bass.ds(e, 1), :],
                                  ALU.add).then_inc(s_y, 1)

            def one(s, b, i):
                turned(s, b)
                if not (isinstance(s, int) and s == 0):
                    result(s - 1, (b - 1) % U, i if b else i - 1)
            dve.wait_ge(s_tab, 1)
            dve.wait_ge(s_w2, 32)
            run_slots(dve, one)
            result(NS - 1, U - 1, NS // U - 1)

            dve.wait_ge(s_gate, 1)

            def combine(c, p, i):
                dve.wait_ge(s_yb[p], (i + 1) * 16 * K)
                for k in range(K):
                    for j in range(G):
                        o = x2[:, bass.ds(c * G + j, 1), :]
                        b = dve.scalar_tensor_tensor(out=o, in0=yback[:, p, k, j:j + 1, :],
                                                     scalar=gate[:, k, bass.ds(c * G + j, 1)], in1=o,
                                                     op0=ALU.mult, op1=ALU.add)
                    b.then_inc([s_o1, s_o][k], 1)
                    if k == 0:
                        dve.wait_ge(s_o1, c + 1)
            with dve.Fori(0, NG // 2) as i:
                combine(i * 2, 0, i)
                combine(i * 2 + 1, 1, i)


NAMES = ["x", "Wq", "bq", "Wk", "bk", "Wv", "bv", "Wo", "bo", "m"]
FFN = ["Wg", "w1", "b1", "w2", "b2"]


def kernel(**inputs):
    import concourse.bacc as bacc
    from concourse.bass_utils import run_bass_kernel_spmd

    nc = bacc.Bacc("TRN2", target_bir_lowering=False, num_devices=1)
    arrays, args = {}, []
    for name in [f"L0_attn_{n}" for n in NAMES] + [f"L0_ffn_{n}" for n in FFN]:
        a = np.ascontiguousarray(inputs[name])
        arrays[f"in_{name}"] = a
        args.append(nc.dram_tensor(f"in_{name}", a.shape, mybir.dt.from_np(a.dtype), kind="ExternalInput").ap())
    nb, s, d = inputs["L0_attn_x"].shape
    e = inputs["L0_ffn_w1"].shape[0]
    args.append(nc.dram_tensor("out", (nb, s, d), F32, kind="ExternalOutput").ap())
    args.append(nc.dram_tensor("xs", (e * (nb * s + P) + P, d + 1), F32).ap())
    args.append(nc.dram_tensor("ys", (2 * nb * s, d), F32).ap())
    moe_block(nc, *args)
    r = run_bass_kernel_spmd(nc, [arrays], core_ids=[0])
    return r.results[0]["out"]
```

```python
from contextlib import ExitStack

import numpy as np
import concourse.bass as bass
from concourse import mybir

P = 128
F32 = mybir.dt.float32
F32R = mybir.dt.float32r
BF16 = mybir.dt.bfloat16
I32 = mybir.dt.int32
ALU = mybir.AluOpType
ACT = mybir.ActivationFunctionType
AX = mybir.AxisListType.X
LN_EPS = 1e-5
L2_EPS = 1e-12


def moe_block(nc, x, Wq, bq, Wk, bk, Wv, bv, Wo, bo, m, Wg, w1, b1, w2, b2, out, xs, ys):
    NB, S, D = x.shape
    HEADS = m.shape[0]
    HD = D // HEADS
    E, _, F = w1.shape
    FC = F // P
    K = 2
    T = NB * S
    NT = T // P
    G = 4
    NG = NT // G
    BG = G * P // S
    TB = S // P
    REGION = T + P
    ROW = D + 1
    NS = K * NT + E
    ESH = (E - 1).bit_length()
    U = 8
    SENT_OUT = K * T
    assert D == P and NS % U == 0 and NG % 2 == 0 and NG >= 4 and E == NG

    x_v = x.rearrange("b (u p) f -> p (b u) f", p=P)
    out_v = out.rearrange("b (u p) f -> p (b u) f", p=P)
    ys_v = ys.rearrange("(k t p) f -> p k t f", k=K, p=P)

    with ExitStack() as ctx:
        def sb(name, shape, dt=F32):
            return ctx.enter_context(nc.sbuf_tensor(name, shape, dt))

        def pb(name, shape, dt=F32):
            return ctx.enter_context(nc.psum_tensor(name, shape, dt))

        def sem(name):
            return ctx.enter_context(nc.semaphore(name))

        xin = sb("xin", [P, NT, D])
        x2 = sb("x2", [P, NT, D])
        w1s = sb("w1s", [P, E, F])
        w1h = sb("w1h", [P, E, F], F32R)
        w1l = sb("w1l", [P, E, F], F32R)
        w2s = sb("w2s", [P, E, FC * D])
        w2hl = sb("w2hl", [P, E, FC * 2 * D], F32R)
        w2p = w2hl[:].rearrange("p e (c h d) -> p e c h d", c=FC, h=2)
        b2bc = sb("b2bc", [P, E, D])
        bobc = sb("bobc", [P, D])
        bocol = sb("bocol", [P, 1])
        wqk = sb("wqk", [P, 2 * D])
        wv = sb("wv", [P, D])
        wog = sb("wog", [P, D + E])
        wgrow = sb("wgrow", [E, D])
        wgT = sb("wgT", [P, E])
        bog = sb("bog", [P, G, E])
        brow = sb("brow", [1, 3 * D])
        ring = sb("ring", [P, E * F])
        b1row = ring[0:1, :].rearrange("p (e f) -> p e f", e=E)
        mcol = sb("mcol", [P, 1])
        ident = sb("ident", [P, P])
        headmask = sb("headmask", [P, P])
        negmean = sb("negmean", [P, P])
        onerow = sb("onerow", [1, P])
        tri = sb("tri", [P, P], BF16)
        ones = sb("ones", [P, P], BF16)
        eps = sb("eps", [P, 1])
        enum = sb("enum", [P, G, K, E])
        enumi = sb("enumi", [P, G, K, E], I32)
        regbase = sb("regbase", [P, G, E])
        regbasei = sb("regbasei", [P, G, E], I32)
        dest = sb("dest", [P, NT, K], I32)
        sidx = sb("sidx", [1, NS])
        sidxi = sb("sidxi", [1, NS], I32)
        padrow = sb("padrow", [P, ROW])
        stats = sb("stats", [P, 2 * G, 6])
        sv = sb("sv", [P, 2 * G, 2])
        md = sb("md", [P, 2 * G])
        var = sb("var", [P, 2 * G])
        std = sb("std", [P, 2 * G])
        rstd = sb("rstd", [P, 2 * G])
        mms = sb("mms", [P, 2 * G])
        shift = sb("shift", [P, 2 * G])
        stdall = sb("stdall", [P, NT])
        rall = sb("rall", [P, NT])
        xn = sb("xn", [P, 2, G, D])
        xnT = sb("xnT", [P, 2, G, P])
        sq = sb("sq", [P, G * 2 * HEADS, HD])
        n2 = sb("n2", [P, G * 2 * HEADS])
        nrm = sb("nrm", [P, G * 2 * HEADS])
        rn = n2
        qk = sb("qk", [P, 2, G, 2 * D])
        qT = sb("qT", [P, G, P])
        xk = sb("xk", [P, BG * D])
        woT, borep = xk[:, 0:D], xk[:, D:2 * D]
        mt = sb("mt", [P, BG * D])
        gm = sb("gm", [P, BG, D + E])
        row = sb("row", [P, 2, G, K, ROW])
        u1 = sb("u1", [P, G, E])
        u2 = sb("u2", [P, G, E])
        u = sb("u", [P, G, E])
        best = sb("best", [P, G, E])
        bestall = sb("bestall", [P, NT, E])
        bidx = sb("bidx", [P, G, E], mybir.dt.uint32)
        bidxf = sb("bidxf", [P, G, K])
        sel = sb("sel", [P, 2, G, K, E])
        mask = sb("mask", [P, G, E], BF16)
        msum = sb("msum", [P, E])
        seen = sb("seen", [P, E], BF16)
        pos = sb("pos", [P, G, E])
        spos = sb("spos", [P, G, K, E])
        slot = sb("slot", [P, 2, G, K], I32)
        cnt = sb("cnt", [1, E])
        cnti = sb("cnti", [1, E], I32)
        tilesi = sb("tilesi", [1, E], I32)
        tiles = sb("tiles", [1, E])
        tend = sb("tend", [1, E])
        tinc = sb("tinc", [1, E])
        esum = sb("esum", [1, NS])
        rsum = sb("rsum", [1, NS])
        etabf = sb("etabf", [1, 1 + NS])
        etab = sb("etab", [1, NS], I32)
        powers = sb("powers", [1, U])
        eshift = sb("eshift", [1, NS // U, U])
        epack = sb("epack", [1, NS // U], I32)
        spare = xin[:].rearrange("p t d -> p (t d)")
        past = spare[0:1, 0:NS * E].rearrange("p (s e) -> p s e", e=E)
        pinc = spare[0:1, NS * E:2 * NS * E].rearrange("p (s e) -> p s e", e=E)
        dlog = spare[:, 2 * NS * E:2 * NS * E + NT * E].rearrange("p (t e) -> p t e", e=E)
        rtab = sb("rtab", [1, NS], I32)
        ptab = sb("ptab", [1, E], I32)
        onee = sb("onee", [1, E])
        scratch = sb("scratch", [1, 2])
        esm = sb("esm", [P, NT])
        gate = sb("gate", [P, K, NT])
        xt = ring[:, 0:U * ROW].rearrange("p (u r) -> p u r", u=U)
        xTh = sb("xTh", [P, 2, P], F32R)
        xTl = sb("xTl", [P, 2, P], F32R)
        h = ring[:, U * ROW:U * ROW + 2 * F].rearrange("p (b f) -> p b f", b=2)
        hTh = sb("hTh", [P, 2, F], F32R)
        hTl = sb("hTl", [P, 2, F], F32R)
        y = ring[:, U * ROW + 2 * F:U * ROW + 2 * F + U * D].rearrange("p (u d) -> p u d", u=U)
        R = 4
        yback = w1s[:].rearrange("p e f -> p (e f)").rearrange("p (r k g d) -> p r k g d", r=R, k=K, g=G)

        psX = pb("psX", [P, 512])
        psQK = pb("psQK", [P, 1024])
        psQ = pb("psQ", [P, 512])
        psKV = pb("psKV", [P, 512])
        psG = pb("psG", [P, 512])
        psO = pb("psO", [P, 512])
        psW = pb("psW", [P, 512])
        psXK, psMT = psKV[:, 0:BG * D], psKV[:, BG * D:2 * BG * D]
        psGM = psG[:, 0:BG * (D + E)].rearrange("p (b f) -> p b f", b=BG)
        psPos = psG[:, 320:320 + G * E].rearrange("p (g e) -> p g e", g=G)
        psCnt = psG[0:1, 384:384 + E]
        psUX = psQ[:, 0:G * E].rearrange("p (g e) -> p g e", g=G)
        psUO = psQ[:, G * E:2 * G * E].rearrange("p (g e) -> p g e", g=G)
        psXT = [psX[:, 0:P], psW[:, 0:P]]
        psH = [psQK[:, 0:F], psQK[:, 512:512 + F]]
        psHT = [psQ, psKV]
        psY = [psO[:, 0:2 * D], psG[:, 0:2 * D]]

        s_xin = [sem(f"s_xin{i}") for i in range(3)]
        s_wa = sem("s_wa")
        s_wb = sem("s_wb")
        s_w2 = sem("s_w2")
        s_b2 = sem("s_b2")
        s_zero = sem("s_zero")
        s_const = sem("s_const")
        s_iota = sem("s_iota")
        s_cf = sem("s_cf")
        s_ea = sem("s_ea")
        s_eb = sem("s_eb")
        s_hm = sem("s_hm")
        s_pw = sem("s_pw")
        s_w = sem("s_w")
        s_ws = sem("s_ws")
        s_bo = sem("s_bo")
        s_w2h = sem("s_w2h")
        s_w2l = sem("s_w2l")
        s_st = sem("s_st")
        s_half = sem("s_half")
        s_var = sem("s_var")
        s_std = sem("s_std")
        s_rstd = sem("s_rstd")
        s_shift = sem("s_shift")
        s_xn = sem("s_xn")
        s_psX = sem("s_psX")
        s_xnT = sem("s_xnT")
        s_psQK = sem("s_psQK")
        s_sq = sem("s_sq")
        s_n2r = sem("s_n2r")
        s_n2 = sem("s_n2")
        s_nrm = sem("s_nrm")
        s_rn = sem("s_rn")
        s_qk = sem("s_qk")
        s_psQ = sem("s_psQ")
        s_psXK = sem("s_psXK")
        s_qT = sem("s_qT")
        s_xk = sem("s_xk")
        s_psMT = sem("s_psMT")
        s_mt = sem("s_mt")
        s_psGM = sem("s_psGM")
        s_gm = sem("s_gm")
        s_psO = sem("s_psO")
        s_xb = sem("s_xb")
        s_x2 = sem("s_x2")
        s_psU = sem("s_psU")
        s_u1 = sem("s_u1")
        s_u2 = sem("s_u2")
        s_u = sem("s_u")
        s_best = sem("s_best")
        s_bidx = sem("s_bidx")
        s_bf = sem("s_bf")
        s_sel = sem("s_sel")
        s_mask = sem("s_mask")
        s_msum = sem("s_msum")
        s_row = sem("s_row")
        s_free = sem("s_free")
        s_psW = sem("s_psW")
        s_w1 = sem("s_w1")
        s_w1h = sem("s_w1h")
        s_w1l = sem("s_w1l")
        s_psPos = sem("s_psPos")
        s_seen = sem("s_seen")
        s_pos = sem("s_pos")
        s_sp = sem("s_sp")
        s_slot = sem("s_slot")
        s_carry = sem("s_carry")
        s_scat = [sem(f"s_scat{i}") for i in range(2)]
        s_cnt = sem("s_cnt")
        s_tb = sem("s_tb")
        s_ptab = sem("s_ptab")
        s_tab = sem("s_tab")
        s_pad = sem("s_pad")
        s_pad2 = sem("s_pad2")
        s_dt = sem("s_dt")
        s_dlog = sem("s_dlog")
        s_elog = sem("s_elog")
        s_gt = sem("s_gt")
        s_gate = sem("s_gate")
        s_xt = [sem(f"s_xt{i}") for i in range(U)]
        s_psXT = sem("s_psXT")
        s_xTh = sem("s_xTh")
        s_xTl = sem("s_xTl")
        s_psH = sem("s_psH")
        s_h = sem("s_h")
        s_psHT = sem("s_psHT")
        s_hTh = sem("s_hTh")
        s_hTl = sem("s_hTl")
        s_psY = sem("s_psY")
        s_yl = sem("s_yl")
        s_y = sem("s_y")
        s_back = [sem(f"s_back{i}") for i in range(U)]
        s_yb = [sem(f"s_yb{i}") for i in range(R)]
        s_o0 = sem("s_o0")
        s_o1 = sem("s_o1")
        s_o = sem("s_o")
        s_out = sem("s_out")

        block = ctx.enter_context(nc.Block())

        def after(eng, s, v):
            if not isinstance(v, int) or v > 0:
                eng.wait_ge(s, v)

        def run_groups(eng, step):
            step(0, None, None, None, False)
            step(1, 0, None, None, True)
            step(2, 1, 0, None, False)
            with eng.Fori(1, NG // 2 - 1) as i:
                step(i * 2 + 1, i * 2, i * 2 - 1, i * 2 - 2, True)
                step(i * 2 + 2, i * 2 + 1, i * 2, i * 2 - 1, False)
            step(NG - 1, NG - 2, NG - 3, NG - 4, True)
            step(None, NG - 1, NG - 2, NG - 3, False)
            step(None, None, NG - 1, NG - 2, True)
            step(None, None, None, NG - 1, False)

        def run_slots(one, eng, packed=False):
            def round(s0, i):
                e = []
                if packed:
                    v = eng.value_load(epack[0:1, bass.ds(i, 1)], min_val=0, max_val=E ** U - 1)
                    e = [(v >> (ESH * j)) & (E - 1) for j in range(U)]
                for b in range(U):
                    one(s0 + b, b, i, e)
            round(0, 0)
            with eng.Fori(1, NS // U - 1) as i:
                round(i * U, i)
            round(NS - U, NS // U - 1)

        def norm_range(gn, gc):
            n = gn + 1 if gn is not None else gc + 4
            return 0 if gn is not None else G, 2 * G if gc is not None else G, n

        def pads(eng, experts, s):
            eng.wait_ge(s_ptab, 1)
            at = [eng.value_load(ptab[0:1, e:e + 1], min_val=0, max_val=E * REGION - P) for e in experts]
            for r in at:
                eng.dma_start(xs[bass.ds(r, P), :], padrow[:]).then_inc(s, 16)

        def tiles_of(t, g):
            return t[:, bass.ds(g * G, G)]

        @block.sync
        def _(sp):
            sp.dma_start(xin[:, 0:G, :], x_v[:, 0:G, :]).then_inc(s_xin[0], 16)
            sp.dma_start(wqk[:, 0:D], Wq).then_inc(s_wa, 16)
            sp.dma_start(wqk[:, D:2 * D], Wk).then_inc(s_wa, 16)
            sp.dma_start(wv[:], Wv).then_inc(s_wa, 16)
            sp.dma_start(xin[:, G:2 * G, :], x_v[:, G:2 * G, :]).then_inc(s_xin[1], 16)
            sp.dma_start(xin[:, 2 * G:NT, :], x_v[:, 2 * G:NT, :]).then_inc(s_xin[2], 16)
            sp.dma_start(w1s[:], w1.rearrange("e d f -> d e f")).then_inc(s_wb, 16)
            sp.dma_start(w2s[:].rearrange("p e (c d) -> p e c d", c=FC),
                         w2.rearrange("e (c p) d -> p e c d", p=P)).then_inc(s_w2, 16)
            sp.dma_start(b2bc[:], b2.partition_broadcast(P)).then_inc(s_b2, 16)
            sp.wait_ge(s_zero, 2)
            sp.dma_start(xs[E * REGION:E * REGION + P, :], padrow[:]).then_inc(s_pad, 16)
            sp.sem_inc(s_free, 2)
            with sp.Fori(0, NG // 2) as i:
                for p in range(2):
                    sp.wait_ge(s_scat[p], (i + 1) * (16 * G * K))
                    sp.sem_inc(s_free, 1)

            pads(sp, range(E // 2), s_pad)
            sp.wait_ge(s_tab, 1)
            sp.wait_ge(s_pad, 16 * (E // 2 + 1))
            sp.wait_ge(s_pad2, 16 * (E - E // 2))

            def load(s, b, i, e):
                after(sp, s_back[b], 16 * i)
                r = sp.value_load(rtab[0:1, bass.ds(s, 1)], min_val=0, max_val=E * REGION)
                sp.dma_start(xt[:, b, :], xs[bass.ds(r, P), :]).then_inc(s_xt[b], 16)
            run_slots(load, sp)

            for b in range(U):
                sp.wait_ge(s_back[b], 16 * (NS // U))
            for c in range(NG):
                if c >= R:
                    sp.wait_ge(s_o, c - R + 1)
                for k in range(K):
                    sp.dma_start(yback[:, c % R, k], ys_v[:, k, c * G:(c + 1) * G, :]).then_inc(s_yb[c % R], 16)
            sp.wait_ge(s_out, 16 * NG)

        @block.gpsimd
        def _(pool):
            pool.memset(ident[:], 0.0)
            pool.memset(negmean[:], -1.0 / D)
            pool.memset(onerow[:], 1.0 / D)
            pool.memset(eps[:], LN_EPS)
            pool.memset(headmask[:], 1.0)
            pool.memset(tri[:], 1.0)
            pool.memset(padrow[:], 0.0)
            pool.memset(ones[:], 1.0)
            pool.memset(onee[:], 1.0)
            pool.memset(scratch[:], 0.0)
            pool.memset(etabf[:], 0.0)
            for j in range(U):
                pool.memset(powers[0:1, j:j + 1], float(E ** j))
            pool.memset(seen[:], 0.0).then_inc(s_zero, 1)
            pool.wait_ge(s_zero, 1)
            pool.affine_select(out=ident[:], in_=ident[:], compare_op=ALU.not_equal, fill=1.0, base=0,
                               pattern=[[-1, P]], channel_multiplier=1)
            pool.affine_select(out=tri[:], in_=tri[:], compare_op=ALU.is_ge, fill=0.0, base=-1,
                               pattern=[[1, P]], channel_multiplier=-1)
            hm = headmask[:].rearrange("p (h d) -> p h d", h=HEADS)
            pool.affine_select(out=hm, in_=hm, compare_op=ALU.is_ge, fill=0.0, base=0,
                               pattern=[[-HD, HEADS], [0, HD]], channel_multiplier=1).then_inc(s_const, 1)
            pool.wait_ge(s_const, 1)
            pool.affine_select(out=hm, in_=hm, compare_op=ALU.is_ge, fill=0.0, base=HD - 1,
                               pattern=[[HD, HEADS], [0, HD]], channel_multiplier=-1).then_inc(s_const, 1)
            pool.iota(padrow[:, D:ROW].bitcast(I32), pattern=[[0, 1]], base=SENT_OUT,
                      channel_multiplier=0).then_inc(s_zero, 1)
            pool.iota(enumi[:], pattern=[[0, G], [0, K], [1, E]], base=0, channel_multiplier=0)
            pool.iota(regbasei[:], pattern=[[0, G], [REGION, E]], base=0, channel_multiplier=0)
            pool.iota(dest[:], pattern=[[P, NT], [T, K]], base=0, channel_multiplier=1)
            pool.iota(sidxi[:], pattern=[[1, NS]], base=0, channel_multiplier=0).then_inc(s_iota, 1)

            pool.wait_ge(s_bo, 32)
            for c in range(3):
                pool.wait_ge(s_xin[c], 16)
                n = G if c < 2 else NT - 2 * G
                t0 = c * G
                for q in range(t0, t0 + n, G):
                    pool.tensor_tensor(x2[:, q:q + G, :], xin[:, q:q + G, :],
                                       bobc[:].unsqueeze(1).to_broadcast([P, G, D]), ALU.add).then_inc(s_xb, 1)
            for e in range(E):
                pool.wait_ge(s_w2h, e + 1)
                pool.tensor_tensor(w2p[:, e, :, 1, :], w2s[:, e, :].rearrange("p (c d) -> p c d", c=FC),
                                   w2p[:, e, :, 0, :].bitcast(F32), ALU.subtract).then_inc(s_w2l, 1)

            xs_bound = pool.to_reg(E * REGION - 1)
            ys_bound = pool.to_reg(K * T - 1)

            def carry_wait(n):
                after(pool, s_carry, n)
                pool.tensor_tensor(scratch[0:1, 1:2], scratch[0:1, 0:1], scratch[0:1, 0:1], ALU.add).then_inc(s_carry, 1)

            def step(gn, ga, gb, gc, even):
                if gc is not None:
                    p = 0 if even else 1
                    pool.wait_ge(s_slot, gc + 1)
                    pool.wait_ge(s_row, gc + 1)
                    carry_wait(gc)
                    for j in range(G):
                        for k in range(K):
                            pool.indirect_dma_start(
                                out=xs, out_offset=bass.IndirectOffsetOnAxis(ap=slot[:, p, j, k:k + 1], axis=0),
                                in_=row[:, p, j, k, :], in_offset=None,
                                bounds_check=xs_bound, oob_is_err=False).then_inc(s_scat[p], 16)
            run_groups(pool, step)

            def put(s, b, i, e):
                pool.wait_ge(s_y, s + 1)
                carry_wait(s + NG)
                pool.indirect_dma_start(
                    out=ys, out_offset=bass.IndirectOffsetOnAxis(ap=xt[:, b, D:ROW].bitcast(I32), axis=0),
                    in_=y[:, b, :], in_offset=None,
                    bounds_check=ys_bound, oob_is_err=False).then_inc(s_back[b], 16)
            run_slots(put, pool)

        @block.tensor
        def _(pe):
            def centred(dst, src, bias):
                mm = pe.matmul(dst, negmean[:], src, start=True, stop=bias is None)
                if bias is not None:
                    mm = pe.matmul(dst, onerow[:], bias, start=False, stop=True)
                return mm

            pe.wait_ge(s_zero, 2)
            pe.wait_ge(s_const, 2)
            pe.wait_ge(s_ea, 16 * 5)
            pe.transpose(psW[:, 0:E], wgrow[:], ident[0:E, 0:E]).then_inc(s_pw, 1)
            pe.transpose(psX[:, 0:D], wog[:, 0:D], ident[:]).then_inc(s_pw, 1)
            pe.wait_ge(s_wa, 16 * 3)
            centred(psQK[:, 0:2 * D], wqk[:], brow[0:1, 0:2 * D]).then_inc(s_pw, 1)
            centred(psO[:, 0:D], wv[:], brow[0:1, 2 * D:3 * D]).then_inc(s_pw, 1)
            pe.wait_ge(s_ws, 1)
            centred(psG[:, 0:E], wgT[:], None).then_inc(s_pw, 1)
            pe.wait_ge(s_w, 3)
            pe.wait_ge(s_ws, 3)
            pe.matmul(psKV[:, 0:E], woT[:], wgT[:], start=True, stop=True)
            pe.matmul(psKV[:, E:2 * E], borep[:], wgT[:], start=True, stop=True).then_inc(s_pw, 1)

            def step(gn, ga, gb, gc, even):
                if ga is not None:
                    p = 0 if even else 1
                    pe.wait_ge(s_xn, ga + 1)
                    after(pe, s_xnT, ga)
                    if isinstance(ga, int) and ga == 0:
                        pe.wait_ge(s_ws, 2)
                    for j in range(G):
                        mm = pe.transpose(psX[:, j * P:(j + 1) * P], xn[:, p, j, :], ident[:])
                    mm.then_inc(s_psX, 1)
                if gb is not None:
                    p = 1 if even else 0
                    pe.wait_ge(s_qk, gb + 1)
                    after(pe, s_mt, gb)
                    if isinstance(gb, int) and gb == 0:
                        pe.wait_ge(s_ws, 5)
                    for b in range(BG):
                        for t in range(TB):
                            mm = pe.matmul(psXK[:, b * D:(b + 1) * D], xn[:, p, b * TB + t, :],
                                           qk[:, p, b * TB + t, D:2 * D], start=t == 0, stop=t == TB - 1)
                    mm.then_inc(s_psXK, 1)
                    after(pe, s_u2, gb)
                    for j in range(G):
                        mm = pe.transpose(psQ[:, j * P:(j + 1) * P], qk[:, p, j, 0:D], ident[:])
                    mm.then_inc(s_psQ, 1)
                if gc is not None:
                    pe.wait_ge(s_mask, gc + 1)
                    after(pe, s_seen, gc)
                    pe.wait_ge(s_gm, gc + 1)
                    pe.matmul(psPos, tri[:], mask[:], start=True, stop=False)
                    for j in range(G - 1):
                        pe.matmul(psPos[:, j + 1:G, :], ones[:], mask[:, j:j + 1, :].to_broadcast([P, G - 1 - j, E]),
                                  start=False, stop=False)
                    pe.matmul(psPos, ones[:], seen[:].unsqueeze(1).to_broadcast([P, G, E]),
                              start=False, stop=True).then_inc(s_psPos, 1)
                if ga is not None:
                    p = 0 if even else 1
                    pe.wait_ge(s_xnT, ga + 1)
                    if isinstance(ga, int) and ga == 0:
                        pe.wait_ge(s_w, 2)
                    after(pe, s_qk, ga)
                    for j in range(G):
                        mm = pe.matmul(psQK[:, j * 2 * D:(j + 1) * 2 * D], xnT[:, p, j, :], wqk[:], start=True, stop=True)
                    mm.then_inc(s_psQK, 1)
                if gb is not None:
                    p = 1 if even else 0
                    pe.wait_ge(s_xk, gb + 1)
                    pe.matmul(psMT, wv[:], xk[:], start=True, stop=True).then_inc(s_psMT, 1)
                    if isinstance(gb, int) and gb == 0:
                        pe.wait_ge(s_wb, 32)
                    after(pe, s_w1, gb)
                    centred(psW[:], w1s[:, bass.ds(gb, 1), :], b1row[0:1, bass.ds(gb, 1), :]).then_inc(s_psW, 1)
                    pe.wait_ge(s_mt, gb + 1)
                    after(pe, s_pos, gb)
                    for b in range(BG):
                        mm = pe.matmul(psGM[:, b, :], mt[:, b * D:(b + 1) * D], wog[:], start=True, stop=True)
                    mm.then_inc(s_psGM, 1)
                    pe.wait_ge(s_qT, gb + 1)
                    for j in range(G):
                        pe.matmul(psUX[:, j, :], xnT[:, p, j, :], wgT[:], start=True, stop=True)
                    pe.wait_ge(s_gm, gb + 1)
                    for j in range(G):
                        mm = pe.matmul(psUO[:, j, :], qT[:, j, :], gm[:, j // TB, D:D + E], start=True, stop=True)
                    mm.then_inc(s_psU, 1)
                    after(pe, s_x2, gb)
                    for j in range(G):
                        mm = pe.matmul(psO[:, j * D:(j + 1) * D], qT[:, j, :], gm[:, j // TB, 0:D],
                                       start=True, stop=True)
                    mm.then_inc(s_psO, 1)
            run_groups(pe, step)

            pe.wait_ge(s_seen, NG)
            pe.wait_ge(s_pos, NG)
            pe.matmul(psCnt, ones[:, 0:1], seen[:], start=True, stop=True).then_inc(s_cnt, 1)

            pe.wait_ge(s_tab, 1)
            pe.wait_ge(s_w1h, E)
            pe.wait_ge(s_w1l, E)
            pe.wait_ge(s_w2l, E)

            def turn_in(s, b, i):
                q = b % 2
                pe.wait_ge(s_xt[b], (i + 1) * 16)
                after(pe, s_xTl, s - 1)
                pe.transpose(psXT[q], xt[:, b, 0:D], ident[:]).then_inc(s_psXT, 1)

            def up(s, b, e):
                q = b % 2
                pe.wait_ge(s_xTl, s + 1)
                after(pe, s_h, s - 1)
                pe.matmul(psH[q], xTh[:, q, :], w1h[:, bass.ds(e, 1), :], start=True, stop=False)
                pe.matmul(psH[q], xTh[:, q, :], w1l[:, bass.ds(e, 1), :], start=False, stop=False)
                pe.matmul(psH[q], xTl[:, q, :], w1h[:, bass.ds(e, 1), :], start=False, stop=True).then_inc(s_psH, 1)

            def turn_h(s, b):
                q = b % 2
                pe.wait_ge(s_h, s + 1)
                after(pe, s_hTl, s - 1)
                for c in range(FC):
                    mm = pe.transpose(psHT[q][:, c * P:(c + 1) * P], h[:, q, c * P:(c + 1) * P], ident[:])
                mm.then_inc(s_psHT, 1)

            def down(s, b, e):
                q = b % 2
                pe.wait_ge(s_hTl, s + 1)
                after(pe, s_y, s - 1)
                for c in range(FC):
                    at, w = slice(c * P, (c + 1) * P), c * 2 * D
                    pe.matmul(psY[q], hTh[:, q, at], w2hl[:, bass.ds(e, 1), w:w + 2 * D], start=c == 0, stop=False)
                for c in range(FC):
                    at, w = slice(c * P, (c + 1) * P), c * 2 * D
                    mm = pe.matmul(psY[q][:, 0:D], hTl[:, q, at], w2hl[:, bass.ds(e, 1), w:w + D],
                                   start=False, stop=c == FC - 1)
                mm.then_inc(s_psY, 1)

            turn_in(0, 0, 0)
            turn_in(1, 1, 0)

            def expert(s):
                return pe.value_load(etab[0:1, bass.ds(s, 1)], min_val=0, max_val=E - 1)

            late = {}

            def one(s, b, i, e):
                static = isinstance(s, int)
                if static and s == 0:
                    up(0, 0, e[1])
                if not (static and s + 2 >= NS):
                    turn_in(s + 2, (b + 2) % U, i + (b + 2) // U)
                if not (static and s + 1 >= NS):
                    up(s + 1, (b + 1) % U, e[b + 2] if b + 2 < U else late[b + 1])
                turn_h(s, b)
                if not (static and s == 0):
                    down(s - 1, (b - 1) % U, e[b])
                if b in (U - 4, U - 3) and not (static and s + 4 >= NS):
                    late[b + 3] = expert(s + 3)
                if static and s == NS - 1:
                    down(s, b, late[U - 1])
            run_slots(one, pe, True)

        @block.scalar
        def _(act):
            act.dma_start(wgrow[:], Wg).then_inc(s_ea, 16)
            act.dma_start(wog[:, 0:D], Wo).then_inc(s_ea, 16)
            act.dma_start(brow[0:1, 0:D], bq.rearrange("(a f) -> a f", a=1)).then_inc(s_ea, 16)
            act.dma_start(brow[0:1, D:2 * D], bk.rearrange("(a f) -> a f", a=1)).then_inc(s_ea, 16)
            act.dma_start(brow[0:1, 2 * D:3 * D], bv.rearrange("(a f) -> a f", a=1)).then_inc(s_ea, 16)
            act.dma_start(bocol[:], bo.rearrange("(f a) -> f a", a=1)).then_inc(s_bo, 16)
            act.dma_start(bobc[:], bo.partition_broadcast(P)).then_inc(s_bo, 16)
            act.dma_start(mcol[:], m.rearrange("(h a) -> h a", a=1).to_broadcast([HEADS, HD])).then_inc(s_hm, 16)
            act.dma_start(b1row[:], b1.rearrange("e f -> (e f)").rearrange("(a e f) -> a e f", a=1, e=E)).then_inc(s_wb, 16)
            act.wait_ge(s_hm, 16)
            act.activation(mcol[:], mcol[:], ACT.Exp, scale=-1.0).then_inc(s_eb, 1)
            act.wait_ge(s_eb, 3)
            act.activation(mcol[:], mcol[:], ACT.Exp, scale=-float(np.log(S))).then_inc(s_eb, 1)

            def step(gn, ga, gb, gc, even):
                if ga is not None:
                    p = 0 if even else 1
                    act.wait_ge(s_psX, ga + 1)
                    act.copy(xnT[:, p], psX[:].rearrange("p (g t) -> p g t", g=G)).then_inc(s_xnT, 1)
                if gb is not None:
                    act.wait_ge(s_psXK, gb + 1)
                    act.copy(xk[:], psXK).then_inc(s_xk, 1)
                    act.wait_ge(s_psQ, gb + 1)
                    act.copy(qT[:], psQ[:].rearrange("p (g t) -> p g t", g=G)).then_inc(s_qT, 1)
                if gn is not None or gc is not None:
                    lo, hi, n = norm_range(gn, gc)
                    act.wait_ge(s_var, n)
                    act.activation(std[:, lo:hi], var[:, lo:hi], ACT.Sqrt, bias=eps[:, 0:1], scale=1.0 / D).then_inc(s_std, 1)
                if ga is not None:
                    act.wait_ge(s_psQK, ga + 1)
                    after(act, s_n2r, ga)
                    act.activation(sq[:].rearrange("p a d -> p (a d)"), psQK[:], ACT.Square).then_inc(s_sq, 1)
                if gb is not None:
                    act.wait_ge(s_psGM, gb + 1)
                    if gn is not None:
                        act.wait_ge(s_shift, n)
                    act.copy(gm[:], psGM).then_inc(s_gm, 1)
                elif gn is not None:
                    act.wait_ge(s_shift, n)
                if gn is not None:
                    for j in range(G):
                        a = act.activation(xn[:, 1 if even else 0, j, :], tiles_of(xin, gn)[:, j, :], ACT.Identity,
                                           bias=shift[:, j:j + 1], scale=rstd[:, j:j + 1])
                    a.then_inc(s_xn, 1)
                if ga is not None:
                    act.wait_ge(s_n2, ga + 1)
                    if gc is not None:
                        act.wait_ge(s_free, gc + 1)
                        act.wait_ge(s_shift, n)
                    act.activation(nrm[:], n2[:], ACT.Sqrt).then_inc(s_nrm, 1)
                elif gc is not None:
                    act.wait_ge(s_free, gc + 1)
                    act.wait_ge(s_shift, n)
                if gc is not None:
                    p = 0 if even else 1
                    for j in range(G):
                        a = act.activation(row[:, p, j, :, 0:D], tiles_of(x2, gc)[:, j:j + 1, :].to_broadcast([P, K, D]),
                                           ACT.Identity, bias=shift[:, G + j:G + j + 1], scale=rstd[:, G + j:G + j + 1])
                    a.then_inc(s_row, 1)
                if isinstance(gn, int) and gn in (1, 2):
                    if gn == 1:
                        act.wait_ge(s_w2, 16)
                    for e in range((gn - 1) * E // 2, gn * E // 2):
                        act.copy(w2p[:, e, :, 0, :], w2s[:, e, :].rearrange("p (c d) -> p c d", c=FC)).then_inc(s_w2h, 1)
                if gb is not None:
                    act.wait_ge(s_w1, gb + 1)
                    act.copy(w1h[:, bass.ds(gb, 1), :], w1s[:, bass.ds(gb, 1), :]).then_inc(s_w1h, 1)
            run_groups(act, step)

            pads(act, range(E // 2, E), s_pad2)
            act.wait_ge(s_dlog, 1)
            act.activation(dlog[:], dlog[:], ACT.Exp).then_inc(s_elog, 1)

            def turned_in(s, b):
                act.wait_ge(s_psXT, s + 1)
                after(act, s_psH, s - 1)
                act.copy(xTh[:, b % 2, :], psXT[b % 2]).then_inc(s_xTh, 1)

            def high(s, b):
                act.wait_ge(s_psHT, s + 1)
                after(act, s_psY, s - 1)
                act.copy(hTh[:, b % 2], psHT[b % 2][:]).then_inc(s_hTh, 1)

            turned_in(0, 0)
            turned_in(1, 1)

            def one(s, b, i, e):
                act.wait_ge(s_psH, s + 1)
                after(act, s_psHT, s - 1)
                act.activation(h[:, b % 2, :], psH[b % 2], ACT.Gelu).then_inc(s_h, 1)
                if not (isinstance(s, int) and s + 2 >= NS):
                    turned_in(s + 2, b)
                high(s, b)
            run_slots(one, act)

            act.wait_ge(s_gate, 1)
            for c in range(NG):
                act.wait_ge(s_yb[c % R], (c // R + 1) * 16 * K)
                for j in range(G):
                    o = yback[:, c % R, 1, j, :]
                    a = act.mul(o, o, gate[:, 1, c * G + j:c * G + j + 1])
                a.then_inc(s_o1, 1)
                if c >= 1:
                    act.wait_ge(s_o, c)
                    act.dma_start(out_v[:, (c - 1) * G:c * G, :], x2[:, (c - 1) * G:c * G, :]).then_inc(s_out, 16)
            act.wait_ge(s_o, NG)
            act.dma_start(out_v[:, NT - G:NT, :], x2[:, NT - G:NT, :]).then_inc(s_out, 16)

        @block.vector
        def _(dve):
            dve.wait_ge(s_iota, 1)
            dve.tensor_copy(enum[:], enumi[:])
            dve.tensor_copy(regbase[:], regbasei[:])
            dve.tensor_copy(sidx[:], sidxi[:]).then_inc(s_cf, 1)
            dve.wait_ge(s_cf, 1)

            dve.wait_ge(s_eb, 1)
            dve.tensor_scalar(mcol[:], mcol[:], 1.0, None, ALU.add).then_inc(s_eb, 1)
            dve.wait_ge(s_eb, 2)
            dve.reciprocal(mcol[:], mcol[:]).then_inc(s_eb, 1)

            def weights():
                dve.wait_ge(s_pw, 1)
                dve.tensor_copy(wgT[:], psW[:, 0:E]).then_inc(s_ws, 1)
                dve.wait_ge(s_pw, 2)
                dve.tensor_copy(woT[:], psX[:, 0:D]).then_inc(s_ws, 1)
                dve.wait_ge(s_bo, 32)
                dve.tensor_copy(borep[:], bocol[:].to_broadcast([P, P])).then_inc(s_ws, 1)
                dve.wait_ge(s_pw, 3)
                dve.tensor_tensor(wqk[:], psQK[:, 0:2 * D], wqk[:], ALU.add).then_inc(s_w, 1)
                dve.wait_ge(s_pw, 4)
                dve.tensor_tensor(wv[:], psO[:, 0:D], wv[:], ALU.add).then_inc(s_w, 1)
                dve.wait_ge(s_pw, 5)
                dve.tensor_tensor(wgT[:], psG[:, 0:E], wgT[:], ALU.add).then_inc(s_w, 1)
                dve.wait_ge(s_pw, 6)
                dve.tensor_copy(wog[:, D:D + E], psKV[:, 0:E]).then_inc(s_ws, 1)
                dve.tensor_copy(bog[:], psKV[:, E:2 * E].unsqueeze(1).to_broadcast([P, G, E])).then_inc(s_ws, 1)
                dve.wait_ge(s_eb, 4)
                dve.wait_ge(s_const, 2)
                dve.tensor_scalar(headmask[:], headmask[:], mcol[:, 0:1], None, ALU.mult).then_inc(s_cf, 1)
                dve.wait_ge(s_cf, 2)
                dve.wait_ge(s_ws, 5)

            def step(gn, ga, gb, gc, even):
                if isinstance(ga, int) and ga == 0:
                    weights()
                normed = gn is not None or gc is not None
                if normed:
                    lo, hi, n = norm_range(gn, gc)
                    if gn is not None:
                        dve.wait_ge(s_xin[min(gn, 2) if isinstance(gn, int) else 2], 16)
                        for j in range(G):
                            b = dve.bn_stats(stats[:, j, :], tiles_of(xin, gn)[:, j, :])
                    if gc is not None:
                        for j in range(G):
                            b = dve.bn_stats(stats[:, G + j, :], tiles_of(x2, gc)[:, j, :])
                    b.then_inc(s_st, 1)
                    dve.wait_ge(s_st, n)
                    dve.tensor_tensor(sv[:, lo:hi], stats[:, lo:hi, 1:3], stats[:, lo:hi, 4:6], ALU.add)
                    dve.tensor_tensor(md[:, lo:hi], stats[:, lo:hi, 1], stats[:, lo:hi, 4], ALU.subtract).then_inc(s_half, 1)
                if gc is not None:
                    dve.wait_ge(s_psPos, gc + 1)
                    dve.tensor_tensor(pos[:], psPos, regbase[:], ALU.add).then_inc(s_pos, 1)
                if normed:
                    dve.wait_ge(s_half, n * 2 - 1)
                    dve.tensor_tensor(md[:, lo:hi], md[:, lo:hi], md[:, lo:hi], ALU.mult).then_inc(s_half, 1)
                if gc is not None:
                    dve.tensor_reduce(msum[:], mask[:].rearrange("p g e -> p e g"), AX, ALU.add).then_inc(s_msum, 1)
                if normed:
                    dve.wait_ge(s_half, n * 2)
                    dve.scalar_tensor_tensor(out=var[:, lo:hi], in0=md[:, lo:hi], scalar=D / 4.0, in1=sv[:, lo:hi, 1],
                                             op0=ALU.mult, op1=ALU.add).then_inc(s_var, 1)
                if gc is not None:
                    p = 0 if even else 1
                    dve.wait_ge(s_pos, gc + 1)
                    dve.tensor_tensor(spos[:], sel[:, p], pos[:].unsqueeze(2).to_broadcast([P, G, K, E]),
                                      ALU.mult).then_inc(s_sp, 1)
                    dve.wait_ge(s_msum, gc + 1)
                    dve.tensor_tensor(seen[:], seen[:], msum[:], ALU.add).then_inc(s_seen, 1)
                    dve.wait_ge(s_sp, gc + 1)
                    dve.wait_ge(s_free, gc + 1)
                    with nc.allow_low_precision(reason="row numbers below 2**24, summed in float32"):
                        dve.tensor_reduce(slot[:, p], spos[:], AX, ALU.add)
                    dve.tensor_copy(row[:, p, :, :, D:ROW].bitcast(I32).rearrange("p g k a -> p g (k a)"),
                                    dest[:, bass.ds(gc * G, G), :]).then_inc(s_slot, 1)
                if normed:
                    dve.wait_ge(s_std, n)
                    dve.reciprocal(rstd[:, lo:hi], std[:, lo:hi])
                    dve.scalar_tensor_tensor(out=mms[:, lo:hi], in0=sv[:, lo:hi, 0], scalar=0.5, in1=std[:, lo:hi],
                                             op0=ALU.mult, op1=ALU.subtract).then_inc(s_rstd, 1)
                    if gn is not None:
                        dve.tensor_copy(tiles_of(stdall, gn), std[:, 0:G])
                    dve.wait_ge(s_rstd, n)
                    dve.scalar_tensor_tensor(out=shift[:, lo:hi], in0=mms[:, lo:hi], scalar=-1.0, in1=rstd[:, lo:hi],
                                             op0=ALU.mult, op1=ALU.mult).then_inc(s_shift, 1)
                    if gc is not None:
                        dve.tensor_copy(tiles_of(rall, gc), rstd[:, G:2 * G])
                if gb is not None:
                    dve.wait_ge(s_psMT, gb + 1)
                    dve.tensor_tensor(mt[:].rearrange("p (b f) -> p b f", b=BG),
                                      psMT.rearrange("p (b f) -> p b f", b=BG),
                                      headmask[:].unsqueeze(1).to_broadcast([P, BG, D]), ALU.mult).then_inc(s_mt, 1)
                if ga is not None:
                    dve.wait_ge(s_sq, ga + 1)
                    dve.tensor_reduce(n2[:], sq[:], AX, ALU.add).then_inc(s_n2r, 1)
                if gb is not None:
                    dve.wait_ge(s_psW, gb + 1)
                    w = w1s[:, bass.ds(gb, 1), :]
                    dve.tensor_tensor(w, psW[:].unsqueeze(1), w, ALU.add).then_inc(s_w1, 1)
                if ga is not None:
                    dve.wait_ge(s_n2r, ga + 1)
                    dve.tensor_scalar(n2[:], n2[:], L2_EPS * L2_EPS, None, ALU.max).then_inc(s_n2, 1)
                if gb is not None:
                    p = 1 if even else 0
                    dve.wait_ge(s_psU, gb + 1)
                    dve.tensor_tensor(u1[:], psUX, tiles_of(stdall, gb).unsqueeze(2).to_broadcast([P, G, E]),
                                      ALU.mult).then_inc(s_u1, 1)
                    dve.wait_ge(s_u1, gb + 1)
                    dve.tensor_tensor(u2[:], psUO, u1[:], ALU.add).then_inc(s_u2, 1)
                    dve.wait_ge(s_u2, gb + 1)
                    dve.tensor_tensor(u[:], u2[:], bog[:], ALU.add).then_inc(s_u, 1)
                    dve.wait_ge(s_psO, gb + 1)
                    dve.wait_ge(s_xb, gb + 1)
                    dve.tensor_tensor(tiles_of(x2, gb), psO[:].rearrange("p (g f) -> p g f", g=G),
                                      tiles_of(x2, gb), ALU.add).then_inc(s_x2, 1)
                    dve.wait_ge(s_u, gb + 1)
                    dve.wait_ge(s_w1h, gb + 1)
                    w = w1s[:, bass.ds(gb, 1), :]
                    dve.tensor_tensor(w1l[:, bass.ds(gb, 1), :], w, w1h[:, bass.ds(gb, 1), :].bitcast(F32),
                                      ALU.subtract).then_inc(s_w1l, 1)
                    for j in range(G):
                        b = dve.max(best[:, j, :], u[:, j, :])
                    b.then_inc(s_best, 1)
                if ga is not None:
                    p = 0 if even else 1
                    dve.wait_ge(s_nrm, ga + 1)
                    dve.reciprocal(rn[:], nrm[:]).then_inc(s_rn, 1)
                    dve.wait_ge(s_rn, ga + 1)
                    if gb is not None:
                        dve.wait_ge(s_best, gb + 1)
                    dve.tensor_tensor(qk[:, p].rearrange("p g (h d) -> p (g h) d", d=HD),
                                      psQK[:].rearrange("p (a d) -> p a d", d=HD),
                                      rn[:].unsqueeze(2).to_broadcast([P, G * 2 * HEADS, HD]), ALU.mult).then_inc(s_qk, 1)
                elif gb is not None:
                    dve.wait_ge(s_best, gb + 1)
                if gb is not None:
                    p = 1 if even else 0
                    for j in range(G):
                        b = dve.max_index(bidx[:, j, :], best[:, j, :], u[:, j, :])
                    b.then_inc(s_bidx, 1)
                    dve.tensor_copy(tiles_of(bestall, gb), best[:])
                    dve.wait_ge(s_bidx, gb + 1)
                    dve.tensor_copy(bidxf[:], bidx[:, :, 0:K]).then_inc(s_bf, 1)
                    dve.wait_ge(s_bf, gb + 1)
                    dve.wait_ge(s_x2, gb + 1)
                    dve.tensor_tensor(sel[:, p], enum[:], bidxf[:].unsqueeze(3).to_broadcast([P, G, K, E]),
                                      ALU.is_equal).then_inc(s_sel, 1)
                    dve.wait_ge(s_sel, gb + 1)
                    dve.tensor_tensor(mask[:], sel[:, p, :, 0, :], sel[:, p, :, 1, :], ALU.add).then_inc(s_mask, 1)
            run_groups(dve, step)

            links = [0]

            def chain(ins):
                links[0] += 1
                ins.then_inc(s_tb, 1)
                dve.wait_ge(s_tb, links[0])
            dve.wait_ge(s_cnt, 1)
            dve.tensor_tensor(ptab[:], psCnt, regbase[0:1, 0, :], ALU.add).then_inc(s_ptab, 1)
            chain(dve.tensor_scalar(cnti[:], psCnt, float(P - 1), None, ALU.add))
            chain(dve.tensor_scalar(tilesi[:], cnti[:], P.bit_length() - 1, None, ALU.logical_shift_right))
            chain(dve.tensor_copy(tiles[:], tilesi[:]))
            dve.tensor_tensor_scan(tend[:], onee[:], tiles[:], 0.0, ALU.mult, ALU.add)
            chain(dve.tensor_scalar(tinc[:], tiles[:], -float(P), float(REGION), ALU.mult, ALU.add))
            chain(dve.tensor_tensor(past[:], sidx[:].unsqueeze(2).to_broadcast([1, NS, E]),
                                    tend[:].unsqueeze(1).to_broadcast([1, NS, E]), ALU.is_ge))
            dve.tensor_reduce(esum[:], past[:], AX, ALU.add)
            chain(dve.tensor_tensor(pinc[:], past[:], tinc[:].unsqueeze(1).to_broadcast([1, NS, E]), ALU.mult))
            dve.tensor_scalar(etabf[0:1, 1:1 + NS], esum[:], float(E - 1), None, ALU.min)
            chain(dve.tensor_reduce(rsum[:], pinc[:], AX, ALU.add))
            dve.tensor_copy(etab[:], etabf[0:1, 1:1 + NS])
            dve.tensor_tensor(eshift[:], etabf[0:1, 0:NS].rearrange("p (i j) -> p i j", j=U),
                              powers[:].unsqueeze(1).to_broadcast([1, NS // U, U]), ALU.mult)
            chain(dve.scalar_tensor_tensor(out=rsum[:], in0=sidx[:], scalar=float(P), in1=rsum[:],
                                           op0=ALU.mult, op1=ALU.add))
            with nc.allow_low_precision(reason="packed numbers below 2**24, summed in float32"):
                dve.tensor_reduce(epack[:], eshift[:], AX, ALU.add)
            dve.tensor_scalar(rtab[:], rsum[:], float(E * REGION), None, ALU.min).then_inc(s_tab, 1)
            dve.tensor_tensor(dlog[:], bestall[:], bestall[:, :, 0:1].to_broadcast([P, NT, E]),
                              ALU.subtract).then_inc(s_dt, 1)
            dve.wait_ge(s_dt, 1)
            dve.tensor_tensor(dlog[:], dlog[:], rall[:].unsqueeze(2).to_broadcast([P, NT, E]),
                              ALU.mult).then_inc(s_dlog, 1)
            dve.wait_ge(s_elog, 1)
            dve.tensor_reduce(esm[:], dlog[:], AX, ALU.add).then_inc(s_gt, 1)
            dve.wait_ge(s_gt, 1)
            dve.reciprocal(gate[:, 0, :], esm[:]).then_inc(s_gt, 1)
            dve.wait_ge(s_gt, 2)
            dve.tensor_tensor(gate[:, 1, :], dlog[:, :, 1], gate[:, 0, :], ALU.mult).then_inc(s_gate, 1)

            def turned_in(s, b):
                dve.wait_ge(s_xTh, s + 1)
                dve.tensor_tensor(xTl[:, b % 2, :], psXT[b % 2], xTh[:, b % 2, :].bitcast(F32),
                                  ALU.subtract).then_inc(s_xTl, 1)

            def low(s, b):
                dve.wait_ge(s_hTh, s + 1)
                dve.tensor_tensor(hTl[:, b % 2], psHT[b % 2][:], hTh[:, b % 2].bitcast(F32),
                                  ALU.subtract).then_inc(s_hTl, 1)

            def result(s, b, i, e):
                dve.wait_ge(s_psY, s + 1)
                after(dve, s_back[b], 16 * i)
                dve.tensor_tensor(y[:, b:b + 1, :], psY[b % 2][:, D:2 * D].unsqueeze(1), b2bc[:, bass.ds(e, 1), :],
                                  ALU.add).then_inc(s_yl, 1)

            def result_high(s, b):
                dve.wait_ge(s_yl, s + 1)
                dve.tensor_tensor(y[:, b, :], psY[b % 2][:, 0:D], y[:, b, :], ALU.add).then_inc(s_y, 1)

            dve.wait_ge(s_tab, 1)
            dve.wait_ge(s_b2, 16)
            turned_in(0, 0)
            turned_in(1, 1)

            def one(s, b, i, e):
                static = isinstance(s, int)
                if not (static and s + 2 >= NS):
                    turned_in(s + 2, b)
                if not (static and s < 2):
                    result_high(s - 2, (b - 2) % U)
                low(s, b)
                if not (static and s == 0):
                    result(s - 1, (b - 1) % U, i if b else i - 1, e[b])
                if static and s == NS - 1:
                    result_high(s - 1, (b - 1) % U)
                    result(s, b, i, dve.value_load(etab[0:1, s:s + 1], min_val=0, max_val=E - 1))
                    result_high(s, b)
            run_slots(one, dve, True)

            for c in range(NG):
                dve.wait_ge(s_yb[c % R], (c // R + 1) * 16 * K)
                for j in range(G):
                    o = x2[:, c * G + j, :]
                    b = dve.scalar_tensor_tensor(out=o, in0=yback[:, c % R, 0, j, :],
                                                 scalar=gate[:, 0, c * G + j:c * G + j + 1], in1=o,
                                                 op0=ALU.mult, op1=ALU.add)
                b.then_inc(s_o0, 1)
                dve.wait_ge(s_o0, c + 1)
                dve.wait_ge(s_o1, c + 1)
                o = x2[:, c * G:(c + 1) * G, :]
                dve.tensor_tensor(o, o, yback[:, c % R, 1], ALU.add).then_inc(s_o, 1)


NAMES = ["x", "Wq", "bq", "Wk", "bk", "Wv", "bv", "Wo", "bo", "m"]
FFN = ["Wg", "w1", "b1", "w2", "b2"]


def kernel(**inputs):
    import concourse.bacc as bacc
    from concourse.bass_utils import run_bass_kernel_spmd

    nc = bacc.Bacc("TRN2", target_bir_lowering=False, num_devices=1)
    arrays, args = {}, []
    for name in [f"L0_attn_{n}" for n in NAMES] + [f"L0_ffn_{n}" for n in FFN]:
        a = np.ascontiguousarray(inputs[name])
        arrays[f"in_{name}"] = a
        args.append(nc.dram_tensor(f"in_{name}", a.shape, mybir.dt.from_np(a.dtype), kind="ExternalInput").ap())
    nb, s, d = inputs["L0_attn_x"].shape
    e = inputs["L0_ffn_w1"].shape[0]
    args.append(nc.dram_tensor("out", (nb, s, d), F32, kind="ExternalOutput").ap())
    args.append(nc.dram_tensor("xs", (e * (nb * s + P) + P, d + 1), F32).ap())
    args.append(nc.dram_tensor("ys", (2 * nb * s, d), F32).ap())
    moe_block(nc, *args)
    r = run_bass_kernel_spmd(nc, [arrays], core_ids=[0])
    return r.results[0]["out"]
```

```python
from contextlib import ExitStack

import numpy as np
import concourse.bass as bass
from concourse import mybir

P = 128
F32 = mybir.dt.float32
F32R = mybir.dt.float32r
BF16 = mybir.dt.bfloat16
I32 = mybir.dt.int32
ALU = mybir.AluOpType
ACT = mybir.ActivationFunctionType
AX = mybir.AxisListType.X
LN_EPS = 1e-5
L2_EPS = 1e-12


def moe_block(nc, x, Wq, bq, Wk, bk, Wv, bv, Wo, bo, m, Wg, w1, b1, w2, b2, out, xs, ys):
    NB, S, D = x.shape
    HEADS = m.shape[0]
    HD = D // HEADS
    E, _, F = w1.shape
    FC = F // P
    K = 2
    T = NB * S
    NT = T // P
    G = 4
    NG = NT // G
    BG = G * P // S
    TB = S // P
    REGION = T + P
    ROW = D + 1
    NS = K * NT + E - 1
    ESH = (E - 1).bit_length()
    U = 8
    NR = (NS + 1) // U
    HALF = U // 2 + 1
    SENT_OUT = K * T
    assert D == P and (NS + 1) % U == 0 and HALF * ESH < 16 and NG % 2 == 0 and NG >= 4 and E == NG

    x_v = x.rearrange("b (u p) f -> p (b u) f", p=P)
    out_v = out.rearrange("b (u p) f -> p (b u) f", p=P)
    ys_v = ys.rearrange("(k t p) f -> p k t f", k=K, p=P)

    with ExitStack() as ctx:
        def sb(name, shape, dt=F32):
            return ctx.enter_context(nc.sbuf_tensor(name, shape, dt))

        def pb(name, shape, dt=F32):
            return ctx.enter_context(nc.psum_tensor(name, shape, dt))

        def sem(name):
            return ctx.enter_context(nc.semaphore(name))

        xin = sb("xin", [P, NT, D])
        x2 = sb("x2", [P, NT, D])
        w1s = sb("w1s", [P, E, F])
        w1h = sb("w1h", [P, E, F], F32R)
        w1l = sb("w1l", [P, E, F], F32R)
        w2s = sb("w2s", [P, E, FC * D])
        w2hl = sb("w2hl", [P, E, FC * 2 * D], F32R)
        w2p = w2hl[:].rearrange("p e (c h d) -> p e c h d", c=FC, h=2)
        b2bc = sb("b2bc", [P, E, D])
        bobc = sb("bobc", [P, D])
        bocol = sb("bocol", [P, 1])
        wqk = sb("wqk", [P, 2 * D])
        wv = sb("wv", [P, D])
        wog = sb("wog", [P, D + E])
        wgrow = sb("wgrow", [E, D])
        wgT = sb("wgT", [P, E])
        bog = sb("bog", [P, G, E])
        brow = sb("brow", [1, 3 * D])
        ring = sb("ring", [P, E * F])
        b1row = ring[0:1, :].rearrange("p (e f) -> p e f", e=E)
        mcol = sb("mcol", [P, 1])
        ident = sb("ident", [P, P])
        headmask = sb("headmask", [P, P])
        negmean = sb("negmean", [P, P])
        onerow = sb("onerow", [1, P])
        tri = sb("tri", [P, P], BF16)
        ones = sb("ones", [P, P], BF16)
        eps = sb("eps", [P, 1])
        warm = sb("warm", [P, 2])
        enum = sb("enum", [P, G, K, E])
        enumi = sb("enumi", [P, G, K, E], I32)
        regbase = sb("regbase", [P, G, E])
        regbasei = sb("regbasei", [P, G, E], I32)
        dest = sb("dest", [P, NT, K], I32)
        sidx = sb("sidx", [1, NS])
        sidxi = sb("sidxi", [1, NS], I32)
        padrow = sb("padrow", [P, ROW])
        stats = sb("stats", [P, 2 * G, 6])
        sv = sb("sv", [P, 2 * G, 2])
        md = sb("md", [P, 2 * G])
        var = sb("var", [P, 2 * G])
        std = sb("std", [P, 2 * G])
        rstd = sb("rstd", [P, 2 * G])
        mms = sb("mms", [P, 2 * G])
        shift = sb("shift", [P, 2 * G])
        stdall = sb("stdall", [P, NT])
        rall = sb("rall", [P, NT])
        xn = sb("xn", [P, 2, G, D])
        xnT = sb("xnT", [P, G, P])
        sq = sb("sq", [P, G * 2 * HEADS, HD])
        n2 = sb("n2", [P, G * 2 * HEADS])
        nrm = sb("nrm", [P, G * 2 * HEADS])
        rn = n2
        qk = sb("qk", [P, 2, G, 2 * D])
        qT = sb("qT", [P, G, P])
        xk = sb("xk", [P, BG * D])
        woT, borep = xk[:, 0:D], xk[:, D:2 * D]
        mt = sb("mt", [P, BG * D])
        gm = sb("gm", [P, BG, D + E])
        row = sb("row", [P, 2, G, K, ROW])
        ux = sb("ux", [P, G, E])
        uxall = sb("uxall", [P, NT, E])
        u = sb("u", [P, G, E])
        best = sb("best", [P, G, E])
        bestall = sb("bestall", [P, NT, E])
        bidx = sb("bidx", [P, G, E], mybir.dt.uint32)
        bidxf = sb("bidxf", [P, G, K])
        sel = sb("sel", [P, 2, G, K, E])
        mask = sb("mask", [P, G, E], BF16)
        msum = sb("msum", [P, E])
        seen = sb("seen", [P, E], BF16)
        pos = sb("pos", [P, G, E])
        spos = sb("spos", [P, G, K, E])
        slot = sb("slot", [P, 2, G, K], I32)
        cnt = sb("cnt", [1, E])
        cnti = sb("cnti", [1, E], I32)
        tilesi = sb("tilesi", [1, E], I32)
        tiles = sb("tiles", [1, E])
        tend = sb("tend", [1, E])
        tinc = sb("tinc", [1, E])
        esum = sb("esum", [1, NS])
        rsum = sb("rsum", [1, NS])
        etabf = sb("etabf", [1, NR * U + HALF])
        powers = sb("powers", [1, HALF])
        eshift = sb("eshift", [1, NR, 2, HALF])
        epack = sb("epack", [1, NR], I32)
        ehalves = epack[:].bitcast(mybir.dt.int16).rearrange("p (i h) -> p i h", h=2)
        spare = xin[:].rearrange("p t d -> p (t d)")
        past = spare[0:1, 0:NS * E].rearrange("p (s e) -> p s e", e=E)
        pinc = spare[0:1, NS * E:2 * NS * E].rearrange("p (s e) -> p s e", e=E)
        dlog = spare[:, 2 * NS * E:2 * NS * E + NT * E].rearrange("p (t e) -> p t e", e=E)
        rtab = sb("rtab", [1, NS], I32)
        ptab = sb("ptab", [1, E], I32)
        onee = sb("onee", [1, E])
        scratch = sb("scratch", [1, 2])
        esm = sb("esm", [P, NT])
        gate = sb("gate", [P, K, NT])
        xt = ring[:, 0:U * ROW].rearrange("p (u r) -> p u r", u=U)
        xTh = sb("xTh", [P, 2, P], F32R)
        xTl = sb("xTl", [P, 2, P], F32R)
        h = ring[:, U * ROW:U * ROW + 2 * F].rearrange("p (b f) -> p b f", b=2)
        hTh = sb("hTh", [P, 2, F], F32R)
        hTl = sb("hTl", [P, 2, F], F32R)
        y = ring[:, U * ROW + 2 * F:U * ROW + 2 * F + U * D].rearrange("p (u d) -> p u d", u=U)
        R = 4
        yback = w1s[:].rearrange("p e f -> p (e f)").rearrange("p (r k g d) -> p r k g d", r=R, k=K, g=G)

        psX = pb("psX", [P, 512])
        psQK = pb("psQK", [P, 1024])
        psQ = pb("psQ", [P, 512])
        psKV = pb("psKV", [P, 512])
        psG = pb("psG", [P, 512])
        psO = pb("psO", [P, 1024])
        psXK, psMT = psKV[:, 0:BG * D], psKV[:, BG * D:2 * BG * D]
        psGM = psG[:, 0:BG * (D + E)].rearrange("p (b f) -> p b f", b=BG)
        psPos = psG[:, 320:320 + G * E].rearrange("p (g e) -> p g e", g=G)
        psCnt = psG[0:1, 384:384 + E]
        psUX = psO[:, 1024 - G * E:1024].rearrange("p (g e) -> p g e", g=G)
        psO4 = psO[:].rearrange("p (a q) -> p a q", a=2)[:, :, 0:2 * (D + E)].rearrange("p a (b f) -> p a b f", b=2)
        psXT = [psX[:, 0:P], psO[:, 512:512 + P]]
        psH = [psQK[:, 0:F], psQK[:, 512:512 + F]]
        psHT = [psQ, psKV]
        psY = [psO[:, 0:2 * D], psG[:, 0:2 * D]]

        s_xin = [sem(f"s_xin{i}") for i in range(3)]
        s_wa = sem("s_wa")
        s_wb = sem("s_wb")
        s_w2 = sem("s_w2")
        s_b2 = sem("s_b2")
        s_zero = sem("s_zero")
        s_const = sem("s_const")
        s_iota = sem("s_iota")
        s_cf = sem("s_cf")
        s_ea = sem("s_ea")
        s_eb = sem("s_eb")
        s_hm = sem("s_hm")
        s_pw = sem("s_pw")
        s_w = sem("s_w")
        s_ws = sem("s_ws")
        s_bo = sem("s_bo")
        s_w2h = sem("s_w2h")
        s_w2l = sem("s_w2l")
        s_st = sem("s_st")
        s_st2 = sem("s_st2")
        s_half = sem("s_half")
        s_var = sem("s_var")
        s_std = sem("s_std")
        s_rstd = sem("s_rstd")
        s_shift = sem("s_shift")
        s_xn = sem("s_xn")
        s_psX = sem("s_psX")
        s_xnT = sem("s_xnT")
        s_psQK = sem("s_psQK")
        s_sq = sem("s_sq")
        s_n2r = sem("s_n2r")
        s_n2 = sem("s_n2")
        s_nrm = sem("s_nrm")
        s_rn = sem("s_rn")
        s_qk = sem("s_qk")
        s_psQ = sem("s_psQ")
        s_psXK = sem("s_psXK")
        s_qT = sem("s_qT")
        s_xk = sem("s_xk")
        s_psMT = sem("s_psMT")
        s_mt = sem("s_mt")
        s_psGM = sem("s_psGM")
        s_gm = sem("s_gm")
        s_psO = sem("s_psO")
        s_xb = sem("s_xb")
        s_x2 = sem("s_x2")
        s_psU = sem("s_psU")
        s_ux = sem("s_ux")
        s_u2 = sem("s_u2")
        s_u = sem("s_u")
        s_best = sem("s_best")
        s_bidx = sem("s_bidx")
        s_bf = sem("s_bf")
        s_sel = sem("s_sel")
        s_mask = sem("s_mask")
        s_msum = sem("s_msum")
        s_row = sem("s_row")
        s_free = sem("s_free")
        s_psW = sem("s_psW")
        s_w1 = sem("s_w1")
        s_w1b = sem("s_w1b")
        s_w1r = sem("s_w1r")
        s_w1h = sem("s_w1h")
        s_w1l = sem("s_w1l")
        s_psPos = sem("s_psPos")
        s_seen = sem("s_seen")
        s_pos = sem("s_pos")
        s_sp = sem("s_sp")
        s_slot = sem("s_slot")
        s_carry = sem("s_carry")
        s_scat = [sem(f"s_scat{i}") for i in range(2)]
        s_cnt = sem("s_cnt")
        s_tb = sem("s_tb")
        s_ptab = sem("s_ptab")
        s_tab = sem("s_tab")
        s_pad = sem("s_pad")
        s_pad2 = sem("s_pad2")
        s_dt = sem("s_dt")
        s_dlog = sem("s_dlog")
        s_elog = sem("s_elog")
        s_gt = sem("s_gt")
        s_gate = sem("s_gate")
        s_xt = [sem(f"s_xt{i}") for i in range(U)]
        s_psXT = sem("s_psXT")
        s_xTh = sem("s_xTh")
        s_xTl = sem("s_xTl")
        s_psH = sem("s_psH")
        s_h = sem("s_h")
        s_psHT = sem("s_psHT")
        s_hTh = sem("s_hTh")
        s_hTl = sem("s_hTl")
        s_psY = sem("s_psY")
        s_yl = sem("s_yl")
        s_y = sem("s_y")
        s_back = [sem(f"s_back{i}") for i in range(U)]
        s_yb = [sem(f"s_yb{i}") for i in range(R)]
        s_o0 = sem("s_o0")
        s_o1 = sem("s_o1")
        s_o = sem("s_o")
        s_out = sem("s_out")

        block = ctx.enter_context(nc.Block())

        def after(eng, s, v):
            if not isinstance(v, int) or v > 0:
                eng.wait_ge(s, v)

        def run_groups(eng, step):
            step(0, None, None, None, None, 0)
            step(1, 0, None, None, None, 1)
            step(2, 1, 0, None, None, 0)
            step(3, 2, 1, 0, None, 1)
            with eng.Fori(2, NG // 2) as i:
                for p in range(2):
                    n = i * 2 + p
                    step(n, n - 1, n - 2, n - 3, n - 4, p)
            step(None, NG - 1, NG - 2, NG - 3, NG - 4, 0)
            step(None, None, NG - 1, NG - 2, NG - 3, 1)
            step(None, None, None, NG - 1, NG - 2, 0)
            step(None, None, None, None, NG - 1, 1)

        def run_slots(one, eng, packed=False):
            def round(s0, i):
                e = []
                if packed:
                    v = eng.value_load(epack[0:1, bass.ds(i, 1)], min_val=0, max_val=(E ** HALF - 1) * (1 + 2 ** 16))
                    e = [(v >> (j // HALF * 16 + j % HALF * ESH)) & (E - 1) for j in range(U + 2)]
                for b in range(U):
                    if not (isinstance(s0, int) and s0 + b >= NS):
                        one(s0 + b, b, i, e)
            round(0, 0)
            with eng.Fori(1, NR - 1) as i:
                round(i * U, i)
            round((NR - 1) * U, NR - 1)

        def norm_range(gn, gd):
            n = gn + 1 if gn is not None else gd + 5
            return 0 if gn is not None else G, 2 * G if gd is not None else G, n

        def prepared(gn):
            first, banks = {1: (0, [psKV, psQ, psO[:, 0:512]]), 2: (3, [psX, psQ, psKV]), 3: (6, [psX, psQ])}[gn]
            return [(first + k, bank) for k, bank in enumerate(banks)]

        def pads(eng, experts, s):
            eng.wait_ge(s_ptab, 1)
            at = [eng.value_load(ptab[0:1, e:e + 1], min_val=0, max_val=E * REGION - P) for e in experts]
            for r in at:
                eng.dma_start(xs[bass.ds(r, P), :], padrow[:]).then_inc(s, 16)

        def tiles_of(t, g):
            return t[:, bass.ds(g * G, G)]

        @block.sync
        def _(sp):
            def vector(v):
                return v.rearrange("(a f) -> a f", a=1)
            sp.dma_start(xin[:, 0:G, :], x_v[:, 0:G, :]).then_inc(s_xin[0], 16)
            sp.dma_start(wgrow[:], Wg).then_inc(s_ea, 16)
            sp.dma_start(wqk[:, 0:D], Wq).then_inc(s_wa, 16)
            sp.dma_start(wqk[:, D:2 * D], Wk).then_inc(s_wa, 16)
            sp.dma_start(brow[0:1, 0:D], vector(bq)).then_inc(s_ea, 16)
            sp.dma_start(brow[0:1, D:2 * D], vector(bk)).then_inc(s_ea, 16)
            sp.dma_start(wog[:, 0:D], Wo).then_inc(s_ea, 16)
            sp.dma_start(brow[0:1, 2 * D:3 * D], vector(bv)).then_inc(s_ea, 16)
            sp.dma_start(wv[:], Wv).then_inc(s_wa, 16)
            sp.dma_start(bocol[:], bo.rearrange("(f a) -> f a", a=1)).then_inc(s_bo, 16)
            sp.dma_start(bobc[:], bo.partition_broadcast(P)).then_inc(s_bo, 16)
            sp.dma_start(xin[:, G:2 * G, :], x_v[:, G:2 * G, :]).then_inc(s_xin[1], 16)
            sp.wait_ge(s_ea, 16 * 5)
            sp.wait_ge(s_wa, 16 * 3)
            sp.wait_ge(s_bo, 16 * 2)
            sp.dma_start(b1row[:], b1.rearrange("e f -> (e f)").rearrange("(a e f) -> a e f", a=1, e=E)).then_inc(s_wb, 16)
            sp.dma_start(w1s[:], w1.rearrange("e d f -> d e f")).then_inc(s_wb, 16)
            sp.dma_start(xin[:, 2 * G:NT, :], x_v[:, 2 * G:NT, :]).then_inc(s_xin[2], 16)
            sp.dma_start(w2s[:].rearrange("p e (c d) -> p e c d", c=FC),
                         w2.rearrange("e (c p) d -> p e c d", p=P)).then_inc(s_w2, 16)
            sp.dma_start(b2bc[:], b2.partition_broadcast(P)).then_inc(s_b2, 16)
            sp.wait_ge(s_zero, 2)
            sp.dma_start(xs[E * REGION:E * REGION + P, :], padrow[:]).then_inc(s_pad, 16)
            sp.sem_inc(s_free, 2)
            with sp.Fori(0, NG // 2 - 1) as i:
                for p in range(2):
                    sp.wait_ge(s_scat[p], (i + 1) * (16 * G * K))
                    sp.sem_inc(s_free, 1)

            pads(sp, range(E // 2), s_pad)
            sp.wait_ge(s_tab, 1)
            sp.wait_ge(s_pad, 16 * (E // 2 + 1))
            sp.wait_ge(s_pad2, 16 * (E - E // 2))
            sp.wait_ge(s_w1r, E)
            for p in range(2):
                sp.wait_ge(s_scat[p], NG // 2 * 16 * G * K)

            def load(s, b, i, e):
                after(sp, s_back[b], 16 * i)
                r = sp.value_load(rtab[0:1, bass.ds(s, 1)], min_val=0, max_val=E * REGION)
                sp.dma_start(xt[:, b, :], xs[bass.ds(r, P), :]).then_inc(s_xt[b], 16)
            run_slots(load, sp)

            for b in range(U):
                sp.wait_ge(s_back[b], 16 * ((NS - 1 - b) // U + 1))
            for c in range(NG):
                if c >= R:
                    sp.wait_ge(s_o, c - R + 1)
                for k in range(K):
                    sp.dma_start(yback[:, c % R, k], ys_v[:, k, c * G:(c + 1) * G, :]).then_inc(s_yb[c % R], 16)
            sp.wait_ge(s_out, 16 * NG)

        @block.gpsimd
        def _(pool):
            pool.memset(ident[:], 0.0)
            pool.memset(negmean[:], -1.0 / D)
            pool.memset(onerow[:], 1.0 / D)
            pool.memset(eps[:], LN_EPS)
            pool.memset(headmask[:], 1.0)
            pool.memset(tri[:], 1.0)
            pool.memset(padrow[:], 0.0)
            pool.memset(ones[:], 1.0)
            pool.memset(onee[:], 1.0)
            pool.memset(scratch[:], 0.0)
            pool.memset(etabf[:], 0.0)
            for j in range(HALF):
                pool.memset(powers[0:1, j:j + 1], float(E ** j))
            pool.memset(seen[:], 0.0).then_inc(s_zero, 1)
            pool.wait_ge(s_zero, 1)
            pool.affine_select(out=ident[:], in_=ident[:], compare_op=ALU.not_equal, fill=1.0, base=0,
                               pattern=[[-1, P]], channel_multiplier=1)
            pool.affine_select(out=tri[:], in_=tri[:], compare_op=ALU.is_ge, fill=0.0, base=-1,
                               pattern=[[1, P]], channel_multiplier=-1)
            hm = headmask[:].rearrange("p (h d) -> p h d", h=HEADS)
            pool.affine_select(out=hm, in_=hm, compare_op=ALU.is_ge, fill=0.0, base=0,
                               pattern=[[-HD, HEADS], [0, HD]], channel_multiplier=1).then_inc(s_const, 1)
            pool.wait_ge(s_const, 1)
            pool.affine_select(out=hm, in_=hm, compare_op=ALU.is_ge, fill=0.0, base=HD - 1,
                               pattern=[[HD, HEADS], [0, HD]], channel_multiplier=-1).then_inc(s_const, 1)
            pool.iota(padrow[:, D:ROW].bitcast(I32), pattern=[[0, 1]], base=SENT_OUT,
                      channel_multiplier=0).then_inc(s_zero, 1)
            pool.iota(enumi[:], pattern=[[0, G], [0, K], [1, E]], base=0, channel_multiplier=0)
            pool.iota(regbasei[:], pattern=[[0, G], [REGION, E]], base=0, channel_multiplier=0)
            pool.iota(dest[:], pattern=[[P, NT], [T, K]], base=0, channel_multiplier=1)
            pool.iota(sidxi[:], pattern=[[1, NS]], base=0, channel_multiplier=0).then_inc(s_iota, 1)

            pool.wait_ge(s_bo, 32)
            for c in range(3):
                if c == 2:
                    pool.wait_ge(s_wb, 32)
                    for e in range(E):
                        pool.tensor_tensor(w1s[0:1, e, :], w1s[0:1, e, :], b1row[0:1, e, :],
                                           ALU.subtract).then_inc(s_w1b, 1)
                pool.wait_ge(s_xin[c], 16)
                n = G if c < 2 else NT - 2 * G
                t0 = c * G
                for q in range(t0, t0 + n, G):
                    pool.tensor_tensor(x2[:, q:q + G, :], xin[:, q:q + G, :],
                                       bobc[:].unsqueeze(1).to_broadcast([P, G, D]), ALU.add).then_inc(s_xb, 1)
            for e in range(E):
                pool.wait_ge(s_w1, e + 1)
                pool.tensor_tensor(w1s[0:1, e, :], w1s[0:1, e, :], b1row[0:1, e, :], ALU.add).then_inc(s_w1r, 1)
            for e in range(E):
                pool.wait_ge(s_w2h, e + 1)
                pool.tensor_tensor(w2p[:, e, :, 1, :], w2s[:, e, :].rearrange("p (c d) -> p c d", c=FC),
                                   w2p[:, e, :, 0, :].bitcast(F32), ALU.subtract).then_inc(s_w2l, 1)

            xs_bound = pool.to_reg(E * REGION - 1)
            ys_bound = pool.to_reg(K * T - 1)

            def carry_wait(n):
                after(pool, s_carry, n)
                pool.tensor_tensor(scratch[0:1, 1:2], scratch[0:1, 0:1], scratch[0:1, 0:1], ALU.add).then_inc(s_carry, 1)

            def step(gn, ga, gb, gc, gd, p):
                if gd is not None:
                    pool.wait_ge(s_slot, gd + 1)
                    pool.wait_ge(s_row, gd + 1)
                    carry_wait(gd)
                    for j in range(G):
                        for k in range(K):
                            pool.indirect_dma_start(
                                out=xs, out_offset=bass.IndirectOffsetOnAxis(ap=slot[:, p, j, k:k + 1], axis=0),
                                in_=row[:, p, j, k, :], in_offset=None,
                                bounds_check=xs_bound, oob_is_err=False).then_inc(s_scat[p], 16)
            run_groups(pool, step)

            def put(s, b, i, e):
                pool.wait_ge(s_y, s + 1)
                carry_wait(s + NG)
                pool.indirect_dma_start(
                    out=ys, out_offset=bass.IndirectOffsetOnAxis(ap=xt[:, b, D:ROW].bitcast(I32), axis=0),
                    in_=y[:, b, :], in_offset=None,
                    bounds_check=ys_bound, oob_is_err=False).then_inc(s_back[b], 16)
            run_slots(put, pool)

        @block.tensor
        def _(pe):
            def centred(dst, src, bias):
                mm = pe.matmul(dst, negmean[:], src, start=True, stop=bias is None)
                if bias is not None:
                    mm = pe.matmul(dst, onerow[:], bias, start=False, stop=True)
                return mm

            pe.wait_ge(s_zero, 2)
            pe.wait_ge(s_const, 2)
            pe.wait_ge(s_ea, 16 * 5)
            pe.transpose(psQ[:, 0:E], wgrow[:], ident[0:E, 0:E]).then_inc(s_pw, 1)
            pe.transpose(psX[:, 0:D], wog[:, 0:D], ident[:]).then_inc(s_pw, 1)
            pe.wait_ge(s_wa, 16 * 3)
            centred(psQK[:, 0:2 * D], wqk[:], brow[0:1, 0:2 * D]).then_inc(s_pw, 1)
            centred(psO[:, 0:D], wv[:], brow[0:1, 2 * D:3 * D]).then_inc(s_pw, 1)
            pe.wait_ge(s_ws, 1)
            centred(psG[:, 0:E], wgT[:], None).then_inc(s_pw, 1)
            pe.wait_ge(s_w, 3)
            pe.wait_ge(s_ws, 3)
            pe.matmul(psKV[:, 0:E], woT[:], wgT[:], start=True, stop=True)
            pe.matmul(psKV[:, E:2 * E], borep[:], wgT[:], start=True, stop=True).then_inc(s_pw, 1)

            def keep_clock(bank, n):
                for _ in range(n):
                    pe.matmul(bank[:, 0:P], ident[:], ident[:], start=True, stop=True)

            def step(gn, ga, gb, gc, gd, p):
                if ga is not None:
                    after(pe, s_xnT, ga)
                    if isinstance(ga, int) and ga == 0:
                        pe.wait_ge(s_ws, 2)
                    if isinstance(ga, int) and ga == 2:
                        pe.wait_ge(s_w1, 6)
                    if gd is not None and gn is not None:
                        keep_clock(psX, 6)
                    pe.wait_ge(s_xn, ga + 1)
                    for j in range(G):
                        mm = pe.transpose(psX[:, j * P:(j + 1) * P], xn[:, 1 - p, j, :], ident[:])
                    mm.then_inc(s_psX, 1)
                if gb is not None:
                    pe.wait_ge(s_qk, gb + 1)
                    after(pe, s_mt, gb)
                    if isinstance(gb, int) and gb == 1:
                        pe.wait_ge(s_w1, 6)
                    if isinstance(gb, int) and gb == 0:
                        pe.wait_ge(s_w1, 1)
                    for b in range(BG):
                        for t in range(TB):
                            mm = pe.matmul(psXK[:, b * D:(b + 1) * D], xn[:, p, b * TB + t, :],
                                           qk[:, p, b * TB + t, D:2 * D], start=t == 0, stop=t == TB - 1)
                    mm.then_inc(s_psXK, 1)
                if gb is not None:
                    after(pe, s_gm, gb)
                elif gd is not None:
                    pe.wait_ge(s_gm, NG)
                def share_of_x():
                    if gb is not None:
                        after(pe, s_x2, gb)
                    for j in range(G):
                        mm = pe.matmul(psUX[:, j, :], xnT[:, j, :], wgT[:], start=True, stop=True)
                    mm.then_inc(s_psU, 1)

                if gd is not None:
                    pe.wait_ge(s_mask, gd + 1)
                    after(pe, s_seen, gd)
                    after(pe, s_pos, gd)
                    pe.matmul(psPos, tri[:], mask[:], start=True, stop=False)
                    for j in range(G - 1):
                        pe.matmul(psPos[:, j + 1:G, :], ones[:], mask[:, j:j + 1, :].to_broadcast([P, G - 1 - j, E]),
                                  start=False, stop=False)
                    pe.matmul(psPos, ones[:], seen[:].unsqueeze(1).to_broadcast([P, G, E]),
                              start=False, stop=True).then_inc(s_psPos, 1)
                if ga is not None:
                    pe.wait_ge(s_xnT, ga + 1)
                    if isinstance(ga, int) and ga == 0:
                        pe.wait_ge(s_w, 3)
                    after(pe, s_qk, ga)
                    for j in range(G):
                        mm = pe.matmul(psQK[:, j * 2 * D:(j + 1) * 2 * D], xnT[:, j, :], wqk[:], start=True, stop=True)
                    mm.then_inc(s_psQK, 1)
                if gb is not None:
                    pe.wait_ge(s_xk, gb + 1)
                    pe.matmul(psMT, wv[:], xk[:], start=True, stop=True).then_inc(s_psMT, 1)
                if ga is not None:
                    share_of_x()
                if gb is not None:
                    after(pe, s_qT, gb)
                    if isinstance(gb, int) and gb == 0:
                        pe.wait_ge(s_w1, 2)
                    for j in range(G):
                        mm = pe.transpose(psQ[:, j * P:(j + 1) * P], qk[:, p, j, 0:D], ident[:])
                    mm.then_inc(s_psQ, 1)
                    pe.wait_ge(s_mt, gb + 1)
                    if gd is not None:
                        pe.wait_ge(s_pos, gd + 1)
                    for b in range(BG):
                        mm = pe.matmul(psGM[:, b, :], mt[:, b * D:(b + 1) * D], wog[:], start=True, stop=True)
                    mm.then_inc(s_psGM, 1)
                    pe.wait_ge(s_qT, gb + 1)
                    pe.wait_ge(s_gm, gb + 1)
                    if isinstance(gb, int) and gb == 0:
                        pe.wait_ge(s_w1, 3)
                    after(pe, s_x2, gb)
                    if ga is not None:
                        pe.wait_ge(s_ux, ga + 1)
                    for j in range(G):
                        mm = pe.matmul(psO4[:, j // 2, j % 2, :], qT[:, j, :], gm[:, j // TB, :], start=True, stop=True)
                    mm.then_inc(s_psO, 1)
                if isinstance(gn, int) and gn in (1, 2, 3):
                    if gb is not None:
                        pe.wait_ge(s_qT, gb + 1)
                    else:
                        pe.wait_ge(s_ws, 5)
                    for e, bank in prepared(gn):
                        pe.wait_ge(s_w1b, e + 1)
                        centred(bank[:], w1s[:, e, :], None).then_inc(s_psW, 1)
                    if gn == 3:
                        pe.wait_ge(s_w1, E)
            run_groups(pe, step)

            pe.wait_ge(s_seen, NG)
            pe.wait_ge(s_pos, NG)
            pe.matmul(psCnt, ones[:, 0:1], seen[:], start=True, stop=True).then_inc(s_cnt, 1)

            pe.wait_ge(s_tab, 1)
            pe.wait_ge(s_w1h, E)
            pe.wait_ge(s_w1l, E)
            pe.wait_ge(s_w2l, E)

            def turn_in(s, b, i):
                q = b % 2
                pe.wait_ge(s_xt[b], (i + 1) * 16)
                after(pe, s_xTl, s - 1)
                pe.transpose(psXT[q], xt[:, b, 0:D], ident[:]).then_inc(s_psXT, 1)

            def up(s, b, e):
                q = b % 2
                pe.wait_ge(s_xTl, s + 1)
                after(pe, s_h, s - 1)
                pe.matmul(psH[q], xTh[:, q, :], w1h[:, bass.ds(e, 1), :], start=True, stop=False)
                pe.matmul(psH[q], xTh[:, q, :], w1l[:, bass.ds(e, 1), :], start=False, stop=False)
                pe.matmul(psH[q], xTl[:, q, :], w1h[:, bass.ds(e, 1), :], start=False, stop=True).then_inc(s_psH, 1)

            def turn_h(s, b):
                q = b % 2
                pe.wait_ge(s_h, s + 1)
                after(pe, s_hTl, s - 1)
                for c in range(FC):
                    mm = pe.transpose(psHT[q][:, c * P:(c + 1) * P], h[:, q, c * P:(c + 1) * P], ident[:])
                mm.then_inc(s_psHT, 1)

            def down(s, b, e):
                q = b % 2
                pe.wait_ge(s_hTl, s + 1)
                after(pe, s_y, s - 1)
                for c in range(FC):
                    at, w = slice(c * P, (c + 1) * P), c * 2 * D
                    pe.matmul(psY[q], hTh[:, q, at], w2hl[:, bass.ds(e, 1), w:w + 2 * D], start=c == 0, stop=False)
                for c in range(FC):
                    at, w = slice(c * P, (c + 1) * P), c * 2 * D
                    mm = pe.matmul(psY[q][:, 0:D], hTl[:, q, at], w2hl[:, bass.ds(e, 1), w:w + D],
                                   start=False, stop=c == FC - 1)
                mm.then_inc(s_psY, 1)

            turn_in(0, 0, 0)
            turn_in(1, 1, 0)

            def one(s, b, i, e):
                static = isinstance(s, int)
                if static and s == 0:
                    up(0, 0, e[1])
                if not (static and s + 2 >= NS):
                    turn_in(s + 2, (b + 2) % U, i + (b + 2) // U)
                if not (static and s + 1 >= NS):
                    up(s + 1, (b + 1) % U, e[b + 2])
                turn_h(s, b)
                if not (static and s == 0):
                    down(s - 1, (b - 1) % U, e[b])
                if static and s == NS - 1:
                    down(s, b, e[b + 1])
            run_slots(one, pe, True)

        @block.scalar
        def _(act):
            act.dma_start(mcol[:], m.rearrange("(h a) -> h a", a=1).to_broadcast([HEADS, HD])).then_inc(s_hm, 16)
            act.wait_ge(s_hm, 16)
            act.activation(mcol[:], mcol[:], ACT.Exp, scale=-1.0).then_inc(s_eb, 1)
            act.wait_ge(s_eb, 3)
            act.activation(mcol[:], mcol[:], ACT.Exp, scale=-float(np.log(S))).then_inc(s_eb, 1)

            def step(gn, ga, gb, gc, gd, p):
                if ga is not None:
                    act.wait_ge(s_psX, ga + 1)
                    act.copy(xnT[:], psX[:].rearrange("p (g t) -> p g t", g=G)).then_inc(s_xnT, 1)
                if gb is not None:
                    act.wait_ge(s_psXK, gb + 1)
                    act.copy(xk[:], psXK).then_inc(s_xk, 1)
                if gn is not None or gd is not None:
                    lo, hi, n = norm_range(gn, gd)
                    act.wait_ge(s_var, n)
                    act.activation(std[:, lo:hi], var[:, lo:hi], ACT.Sqrt, bias=eps[:, 0:1], scale=1.0 / D).then_inc(s_std, 1)
                if ga is not None:
                    act.wait_ge(s_psQK, ga + 1)
                    after(act, s_n2r, ga)
                    act.activation(sq[:].rearrange("p a d -> p (a d)"), psQK[:], ACT.Square).then_inc(s_sq, 1)
                if gb is not None:
                    act.wait_ge(s_psQ, gb + 1)
                    act.copy(qT[:], psQ[:].rearrange("p (g t) -> p g t", g=G)).then_inc(s_qT, 1)
                    act.wait_ge(s_psGM, gb + 1)
                    if gn is not None:
                        act.wait_ge(s_shift, n)
                    act.copy(gm[:], psGM).then_inc(s_gm, 1)
                elif gn is not None:
                    act.wait_ge(s_shift, n)
                if ga is not None:
                    act.wait_ge(s_n2, ga + 1)
                    act.activation(nrm[:], n2[:], ACT.Sqrt).then_inc(s_nrm, 1)
                if gn is not None:
                    for j in range(G):
                        a = act.activation(xn[:, p, j, :], tiles_of(xin, gn)[:, j, :], ACT.Identity,
                                           bias=shift[:, j:j + 1], scale=rstd[:, j:j + 1])
                    a.then_inc(s_xn, 1)
                if gd is not None:
                    act.wait_ge(s_free, gd + 1)
                    if gn is None:
                        act.wait_ge(s_shift, n)
                    act.copy(warm[:, 0:1], eps[:])
                if gd is not None:
                    for j in range(G):
                        a = act.activation(row[:, p, j, :, 0:D], tiles_of(x2, gd)[:, j:j + 1, :].to_broadcast([P, K, D]),
                                           ACT.Identity, bias=shift[:, G + j:G + j + 1], scale=rstd[:, G + j:G + j + 1])
                    a.then_inc(s_row, 1)
                if isinstance(gc, int) and gc >= NG - 2:
                    for e in range((gc - NG + 2) * E // 2, (gc - NG + 3) * E // 2):
                        act.wait_ge(s_w1r, e + 1)
                        act.copy(w1h[:, e, :], w1s[:, e, :]).then_inc(s_w1h, 1)
                if isinstance(gn, int) and gn in (2, 3):
                    if gn == 2:
                        act.wait_ge(s_w2, 16)
                    for e in range((gn - 2) * E // 2, (gn - 1) * E // 2):
                        act.copy(w2p[:, e, :, 0, :], w2s[:, e, :].rearrange("p (c d) -> p c d", c=FC)).then_inc(s_w2h, 1)
            run_groups(act, step)

            pads(act, range(E // 2, E), s_pad2)
            act.wait_ge(s_dlog, 1)
            act.activation(dlog[:], dlog[:], ACT.Exp).then_inc(s_elog, 1)
            act.activation(warm[:, 1:2], eps[:], ACT.Gelu)

            def turned_in(s, b):
                act.wait_ge(s_psXT, s + 1)
                after(act, s_psH, s - 1)
                act.copy(xTh[:, b % 2, :], psXT[b % 2]).then_inc(s_xTh, 1)

            def high(s, b):
                act.wait_ge(s_psHT, s + 1)
                after(act, s_psY, s - 1)
                act.copy(hTh[:, b % 2], psHT[b % 2][:]).then_inc(s_hTh, 1)

            turned_in(0, 0)
            turned_in(1, 1)

            def one(s, b, i, e):
                act.wait_ge(s_psH, s + 1)
                after(act, s_psHT, s - 1)
                act.activation(h[:, b % 2, :], psH[b % 2], ACT.Gelu).then_inc(s_h, 1)
                if not (isinstance(s, int) and s + 2 >= NS):
                    turned_in(s + 2, b)
                high(s, b)
            run_slots(one, act)

            act.wait_ge(s_gate, 1)
            for c in range(NG):
                act.wait_ge(s_yb[c % R], (c // R + 1) * 16 * K)
                for j in range(G):
                    o = yback[:, c % R, 1, j, :]
                    a = act.mul(o, o, gate[:, 1, c * G + j:c * G + j + 1])
                a.then_inc(s_o1, 1)
                if c >= 1:
                    act.wait_ge(s_o, c)
                    act.dma_start(out_v[:, (c - 1) * G:c * G, :], x2[:, (c - 1) * G:c * G, :]).then_inc(s_out, 16)
            act.wait_ge(s_o, NG)
            act.dma_start(out_v[:, NT - G:NT, :], x2[:, NT - G:NT, :]).then_inc(s_out, 16)

        @block.vector
        def _(dve):
            dve.wait_ge(s_iota, 1)
            dve.tensor_copy(enum[:], enumi[:])
            dve.tensor_copy(regbase[:], regbasei[:])
            dve.tensor_copy(sidx[:], sidxi[:]).then_inc(s_cf, 1)
            dve.wait_ge(s_cf, 1)

            dve.wait_ge(s_eb, 1)
            dve.tensor_scalar(mcol[:], mcol[:], 1.0, None, ALU.add).then_inc(s_eb, 1)
            dve.wait_ge(s_eb, 2)
            dve.reciprocal(mcol[:], mcol[:]).then_inc(s_eb, 1)

            def weights():
                dve.wait_ge(s_pw, 1)
                dve.tensor_copy(wgT[:], psQ[:, 0:E]).then_inc(s_ws, 1)
                dve.wait_ge(s_pw, 2)
                dve.tensor_copy(woT[:], psX[:, 0:D]).then_inc(s_ws, 1)
                dve.wait_ge(s_bo, 32)
                dve.tensor_copy(borep[:], bocol[:].to_broadcast([P, P])).then_inc(s_ws, 1)
                dve.wait_ge(s_pw, 3)
                dve.tensor_tensor(wqk[:], psQK[:, 0:2 * D], wqk[:], ALU.add).then_inc(s_w, 1)
                dve.wait_ge(s_pw, 4)
                dve.tensor_tensor(wv[:], psO[:, 0:D], wv[:], ALU.add).then_inc(s_w, 1)
                dve.wait_ge(s_pw, 5)
                dve.tensor_tensor(wgT[:], psG[:, 0:E], wgT[:], ALU.add).then_inc(s_w, 1)
                dve.wait_ge(s_pw, 6)
                dve.tensor_copy(wog[:, D:D + E], psKV[:, 0:E]).then_inc(s_ws, 1)
                dve.tensor_copy(bog[:], psKV[:, E:2 * E].unsqueeze(1).to_broadcast([P, G, E])).then_inc(s_ws, 1)
                dve.wait_ge(s_eb, 4)
                dve.wait_ge(s_const, 2)
                dve.tensor_scalar(headmask[:], headmask[:], mcol[:, 0:1], None, ALU.mult).then_inc(s_cf, 1)
                dve.wait_ge(s_cf, 2)
                dve.wait_ge(s_ws, 5)

            def step(gn, ga, gb, gc, gd, p):
                def stats_of_x2(*which):
                    if gc is not None:
                        for j in which:
                            b = dve.bn_stats(stats[:, G + j, :], tiles_of(x2, gc)[:, j, :])
                            if j == G - 1:
                                b.then_inc(s_st2, 1)
                if isinstance(ga, int) and ga == 0:
                    weights()
                normed = gn is not None or gd is not None
                if normed:
                    lo, hi, n = norm_range(gn, gd)
                    if gn is not None:
                        if isinstance(gn, int):
                            dve.wait_ge(s_xin[min(gn, 2)], 16)
                        for j in range(G):
                            b = dve.bn_stats(stats[:, j, :], tiles_of(xin, gn)[:, j, :])
                        b.then_inc(s_st, 1)
                if gc is not None:
                    dve.wait_ge(s_psO, gc + 1)
                    dve.tensor_tensor(u[:].rearrange("p (a b) e -> p a b e", a=2), psO4[:, :, :, D:D + E],
                                      tiles_of(uxall, gc).rearrange("p (a b) e -> p a b e", a=2), ALU.add).then_inc(s_u, 1)
                if normed:
                    if gn is not None:
                        dve.wait_ge(s_st, gn + 1)
                    if gd is not None:
                        dve.wait_ge(s_st2, gd + 1)
                    dve.tensor_tensor(sv[:, lo:hi], stats[:, lo:hi, 1:3], stats[:, lo:hi, 4:6], ALU.add)
                    dve.tensor_tensor(md[:, lo:hi], stats[:, lo:hi, 1], stats[:, lo:hi, 4], ALU.subtract).then_inc(s_half, 1)
                if gc is not None:
                    dve.wait_ge(s_xb, gc + 1)
                    dve.wait_ge(s_u, gc + 1)
                    x2g = tiles_of(x2, gc).rearrange("p (a b) d -> p a b d", a=2)
                    dve.tensor_tensor(x2g, psO4[:, :, :, 0:D], x2g, ALU.add).then_inc(s_x2, 1)
                    for j in range(G):
                        b = dve.max(best[:, j, :], u[:, j, :])
                    b.then_inc(s_best, 1)
                if normed:
                    dve.wait_ge(s_half, n * 2 - 1)
                    dve.tensor_tensor(md[:, lo:hi], md[:, lo:hi], md[:, lo:hi], ALU.mult).then_inc(s_half, 1)
                if normed:
                    dve.wait_ge(s_half, n * 2)
                    if gc is not None:
                        dve.wait_ge(s_best, gc + 1)
                    dve.scalar_tensor_tensor(out=var[:, lo:hi], in0=md[:, lo:hi], scalar=D / 4.0, in1=sv[:, lo:hi, 1],
                                             op0=ALU.mult, op1=ALU.add).then_inc(s_var, 1)
                if gc is not None:
                    for j in range(G):
                        b = dve.max_index(bidx[:, j, :], best[:, j, :], u[:, j, :])
                    b.then_inc(s_bidx, 1)
                    dve.tensor_copy(tiles_of(bestall, gc), best[:])
                if gd is not None:
                    dve.wait_ge(s_psPos, gd + 1)
                    dve.tensor_tensor(pos[:], psPos, regbase[:], ALU.add).then_inc(s_pos, 1)
                if gd is not None:
                    dve.tensor_reduce(msum[:], mask[:].rearrange("p g e -> p e g"), AX, ALU.add).then_inc(s_msum, 1)
                    dve.wait_ge(s_pos, gd + 1)
                    dve.tensor_tensor(spos[:], sel[:, p], pos[:].unsqueeze(2).to_broadcast([P, G, K, E]),
                                      ALU.mult).then_inc(s_sp, 1)
                if gc is not None:
                    dve.wait_ge(s_bidx, gc + 1)
                    dve.tensor_copy(bidxf[:], bidx[:, :, 0:K]).then_inc(s_bf, 1)
                if gd is not None:
                    dve.wait_ge(s_msum, gd + 1)
                    dve.tensor_tensor(seen[:], seen[:], msum[:], ALU.add).then_inc(s_seen, 1)
                    dve.wait_ge(s_sp, gd + 1)
                    dve.wait_ge(s_free, gd + 1)
                    with nc.allow_low_precision(reason="row numbers below 2**24, summed in float32"):
                        dve.tensor_reduce(slot[:, p], spos[:], AX, ALU.add)
                    dve.tensor_copy(row[:, p, :, :, D:ROW].bitcast(I32).rearrange("p g k a -> p g (k a)"),
                                    dest[:, bass.ds(gd * G, G), :]).then_inc(s_slot, 1)
                if normed:
                    dve.wait_ge(s_std, n)
                    dve.reciprocal(rstd[:, lo:hi], std[:, lo:hi])
                    dve.scalar_tensor_tensor(out=mms[:, lo:hi], in0=sv[:, lo:hi, 0], scalar=0.5, in1=std[:, lo:hi],
                                             op0=ALU.mult, op1=ALU.subtract).then_inc(s_rstd, 1)
                    if gn is not None:
                        dve.tensor_copy(tiles_of(stdall, gn), std[:, 0:G])
                if gc is not None:
                    dve.wait_ge(s_bf, gc + 1)
                    dve.wait_ge(s_x2, gc + 1)
                    dve.tensor_tensor(sel[:, 1 - p], enum[:], bidxf[:].unsqueeze(3).to_broadcast([P, G, K, E]),
                                      ALU.is_equal).then_inc(s_sel, 1)
                if normed:
                    dve.wait_ge(s_rstd, n)
                    dve.scalar_tensor_tensor(out=shift[:, lo:hi], in0=mms[:, lo:hi], scalar=-1.0, in1=rstd[:, lo:hi],
                                             op0=ALU.mult, op1=ALU.mult).then_inc(s_shift, 1)
                    if gd is not None:
                        dve.tensor_copy(tiles_of(rall, gd), rstd[:, G:2 * G])
                if gc is not None:
                    dve.wait_ge(s_sel, gc + 1)
                    dve.tensor_tensor(mask[:], sel[:, 1 - p, :, 0, :], sel[:, 1 - p, :, 1, :], ALU.add).then_inc(s_mask, 1)
                if gb is not None:
                    dve.wait_ge(s_psMT, gb + 1)
                    dve.tensor_tensor(mt[:].rearrange("p (b f) -> p b f", b=BG),
                                      psMT.rearrange("p (b f) -> p b f", b=BG),
                                      headmask[:].unsqueeze(1).to_broadcast([P, BG, D]), ALU.mult).then_inc(s_mt, 1)
                if ga is not None:
                    dve.wait_ge(s_psU, ga + 1)
                    dve.tensor_tensor(ux[:], psUX, tiles_of(stdall, ga).unsqueeze(2).to_broadcast([P, G, E]),
                                      ALU.mult).then_inc(s_ux, 1)
                if ga is not None:
                    stats_of_x2(0)
                    dve.wait_ge(s_sq, ga + 1)
                    dve.tensor_reduce(n2[:], sq[:], AX, ALU.add).then_inc(s_n2r, 1)
                    dve.wait_ge(s_n2r, ga + 1)
                    dve.tensor_scalar(n2[:], n2[:], L2_EPS * L2_EPS, None, ALU.max).then_inc(s_n2, 1)
                    dve.wait_ge(s_ux, ga + 1)
                    dve.tensor_tensor(tiles_of(uxall, ga), ux[:], bog[:], ALU.add).then_inc(s_u2, 1)
                    dve.wait_ge(s_u2, ga + 1)
                    stats_of_x2(1, 2)
                    dve.wait_ge(s_nrm, ga + 1)
                    dve.reciprocal(rn[:], nrm[:]).then_inc(s_rn, 1)
                    stats_of_x2(3)
                    dve.wait_ge(s_rn, ga + 1)
                    dve.tensor_tensor(qk[:, 1 - p].rearrange("p g (h d) -> p (g h) d", d=HD),
                                      psQK[:].rearrange("p (a d) -> p a d", d=HD),
                                      rn[:].unsqueeze(2).to_broadcast([P, G * 2 * HEADS, HD]), ALU.mult).then_inc(s_qk, 1)
                else:
                    stats_of_x2(*range(G))
                if isinstance(gn, int) and gn in (1, 2, 3):
                    for e, bank in prepared(gn):
                        dve.wait_ge(s_psW, e + 1)
                        dve.tensor_tensor(w1s[:, e, :], bank[:], w1s[:, e, :],
                                          ALU.add).then_inc(s_w1, 1)
            run_groups(dve, step)

            links = [0]

            def chain(ins):
                links[0] += 1
                ins.then_inc(s_tb, 1)
                dve.wait_ge(s_tb, links[0])
            dve.wait_ge(s_cnt, 1)
            dve.tensor_tensor(ptab[:], psCnt, regbase[0:1, 0, :], ALU.add).then_inc(s_ptab, 1)
            chain(dve.tensor_scalar(cnti[:], psCnt, float(P - 1), None, ALU.add))
            chain(dve.tensor_scalar(tilesi[:], cnti[:], P.bit_length() - 1, None, ALU.logical_shift_right))
            chain(dve.tensor_copy(tiles[:], tilesi[:]))
            dve.tensor_tensor_scan(tend[:], onee[:], tiles[:], 0.0, ALU.mult, ALU.add)
            chain(dve.tensor_scalar(tinc[:], tiles[:], -float(P), float(REGION), ALU.mult, ALU.add))
            chain(dve.tensor_tensor(past[:], sidx[:].unsqueeze(2).to_broadcast([1, NS, E]),
                                    tend[:].unsqueeze(1).to_broadcast([1, NS, E]), ALU.is_ge))
            dve.tensor_reduce(esum[:], past[:], AX, ALU.add)
            chain(dve.tensor_tensor(pinc[:], past[:], tinc[:].unsqueeze(1).to_broadcast([1, NS, E]), ALU.mult))
            dve.tensor_scalar(etabf[0:1, 1:1 + NS], esum[:], float(E - 1), None, ALU.min)
            chain(dve.tensor_reduce(rsum[:], pinc[:], AX, ALU.add))
            for half in range(2):
                digits = etabf[0:1, half * HALF:half * HALF + NR * U].rearrange("p (i j) -> p i j", j=U)[:, :, 0:HALF]
                dve.tensor_tensor(eshift[:, :, half, :], digits,
                                  powers[:].unsqueeze(1).to_broadcast([1, NR, HALF]), ALU.mult)
            chain(dve.scalar_tensor_tensor(out=rsum[:], in0=sidx[:], scalar=float(P), in1=rsum[:],
                                           op0=ALU.mult, op1=ALU.add))
            with nc.allow_low_precision(reason="packed numbers below 2**15, summed in float32"):
                dve.tensor_reduce(ehalves, eshift[:], AX, ALU.add)
            dve.tensor_scalar(rtab[:], rsum[:], float(E * REGION), None, ALU.min).then_inc(s_tab, 1)
            for e in range(E):
                dve.wait_ge(s_w1h, e + 1)
                dve.tensor_tensor(w1l[:, e, :], w1s[:, e, :], w1h[:, e, :].bitcast(F32), ALU.subtract).then_inc(s_w1l, 1)
            dve.tensor_tensor(dlog[:], bestall[:], bestall[:, :, 0:1].to_broadcast([P, NT, E]),
                              ALU.subtract).then_inc(s_dt, 1)
            dve.wait_ge(s_dt, 1)
            dve.tensor_tensor(dlog[:], dlog[:], rall[:].unsqueeze(2).to_broadcast([P, NT, E]),
                              ALU.mult).then_inc(s_dlog, 1)
            dve.wait_ge(s_elog, 1)
            dve.tensor_reduce(esm[:], dlog[:], AX, ALU.add).then_inc(s_gt, 1)
            dve.wait_ge(s_gt, 1)
            dve.reciprocal(gate[:, 0, :], esm[:]).then_inc(s_gt, 1)
            dve.wait_ge(s_gt, 2)
            dve.tensor_tensor(gate[:, 1, :], dlog[:, :, 1], gate[:, 0, :], ALU.mult).then_inc(s_gate, 1)

            def turned_in(s, b):
                dve.wait_ge(s_xTh, s + 1)
                dve.tensor_tensor(xTl[:, b % 2, :], psXT[b % 2], xTh[:, b % 2, :].bitcast(F32),
                                  ALU.subtract).then_inc(s_xTl, 1)

            def low(s, b):
                dve.wait_ge(s_hTh, s + 1)
                dve.tensor_tensor(hTl[:, b % 2], psHT[b % 2][:], hTh[:, b % 2].bitcast(F32),
                                  ALU.subtract).then_inc(s_hTl, 1)

            def result(s, b, i, e):
                dve.wait_ge(s_psY, s + 1)
                after(dve, s_back[b], 16 * i)
                dve.tensor_tensor(y[:, b:b + 1, :], psY[b % 2][:, D:2 * D].unsqueeze(1), b2bc[:, bass.ds(e, 1), :],
                                  ALU.add).then_inc(s_yl, 1)

            def result_high(s, b):
                dve.wait_ge(s_yl, s + 1)
                dve.tensor_tensor(y[:, b, :], psY[b % 2][:, 0:D], y[:, b, :], ALU.add).then_inc(s_y, 1)

            dve.wait_ge(s_tab, 1)
            dve.wait_ge(s_b2, 16)
            turned_in(0, 0)
            turned_in(1, 1)

            def one(s, b, i, e):
                static = isinstance(s, int)
                if not (static and s + 2 >= NS):
                    turned_in(s + 2, b)
                if not (static and s < 2):
                    result_high(s - 2, (b - 2) % U)
                low(s, b)
                if not (static and s == 0):
                    result(s - 1, (b - 1) % U, i if b else i - 1, e[b])
                if static and s == NS - 1:
                    result_high(s - 1, (b - 1) % U)
                    result(s, b, i, e[b + 1])
                    result_high(s, b)
            run_slots(one, dve, True)

            for c in range(NG):
                dve.wait_ge(s_yb[c % R], (c // R + 1) * 16 * K)
                for j in range(G):
                    o = x2[:, c * G + j, :]
                    b = dve.scalar_tensor_tensor(out=o, in0=yback[:, c % R, 0, j, :],
                                                 scalar=gate[:, 0, c * G + j:c * G + j + 1], in1=o,
                                                 op0=ALU.mult, op1=ALU.add)
                b.then_inc(s_o0, 1)
                dve.wait_ge(s_o0, c + 1)
                dve.wait_ge(s_o1, c + 1)
                o = x2[:, c * G:(c + 1) * G, :]
                dve.tensor_tensor(o, o, yback[:, c % R, 1], ALU.add).then_inc(s_o, 1)


NAMES = ["x", "Wq", "bq", "Wk", "bk", "Wv", "bv", "Wo", "bo", "m"]
FFN = ["Wg", "w1", "b1", "w2", "b2"]


def kernel(**inputs):
    import concourse.bacc as bacc
    from concourse.bass_utils import run_bass_kernel_spmd

    nc = bacc.Bacc("TRN2", target_bir_lowering=False, num_devices=1)
    arrays, args = {}, []
    for name in [f"L0_attn_{n}" for n in NAMES] + [f"L0_ffn_{n}" for n in FFN]:
        a = np.ascontiguousarray(inputs[name])
        arrays[f"in_{name}"] = a
        args.append(nc.dram_tensor(f"in_{name}", a.shape, mybir.dt.from_np(a.dtype), kind="ExternalInput").ap())
    nb, s, d = inputs["L0_attn_x"].shape
    e = inputs["L0_ffn_w1"].shape[0]
    args.append(nc.dram_tensor("out", (nb, s, d), F32, kind="ExternalOutput").ap())
    args.append(nc.dram_tensor("xs", (e * (nb * s + P) + P, d + 1), F32).ap())
    args.append(nc.dram_tensor("ys", (2 * nb * s, d), F32).ap())
    moe_block(nc, *args)
    r = run_bass_kernel_spmd(nc, [arrays], core_ids=[0])
    return r.results[0]["out"]
```
